# Optimizing a Trainium2 kernel written in Bass

```python
import numpy as np
import jax
import jax.numpy as jnp

def _softmax(x, axis=-1):
    return jax.nn.softmax(x, axis=axis)

def _gelu(x):
    return jax.nn.gelu(x, approximate=True)

def _silu(x):
    return jax.nn.silu(x)

def _sigmoid(x):
    return jax.nn.sigmoid(x)

def _layernorm(x, axis=-1, eps=1e-05):
    m = jnp.mean(x, axis=axis, keepdims=True)
    v = jnp.var(x, axis=axis, keepdims=True)
    return (x - m) / jnp.sqrt(v + eps)

def _scatter_add(tgt, idx, src, axis=0):
    return tgt.at[idx].add(src)

def _segment_sum(src, seg, n):
    return jax.ops.segment_sum(src, seg, n)
kernel_name = 'mk_cond_resid_d2_seqx_r4_da0455'

def setup_inputs(seed: int=0):
    np.random.seed(seed)
    _w = jnp.asarray

    def _rec_inputs():
        import jax
        import jax.numpy as jnp
        _rk = jax.random.key(seed)
        x = -0.000125 + 0.9999 * jax.random.normal(jax.random.fold_in(_rk, 1), (2, 1024, 256), jnp.float32)
        _lenS = 1024 - jax.random.randint(jax.random.fold_in(_rk, 7), (2,), 0, max(1, 1024 // 4) + 1, jnp.int32)
        _lenS2 = 1024 - jax.random.randint(jax.random.fold_in(_rk, 8), (2,), 0, max(1, 1024 // 4) + 1, jnp.int32)
        cond_1024 = -0.00493535 + 1.00056 * jax.random.normal(jax.random.fold_in(_rk, 11), (2, 256), jnp.float32)
        return (x, cond_1024)
    x, cond_1024 = _rec_inputs()

    def _L0_cond_setup():
        import jax, jax.numpy as jnp
        import numpy as np
        import math
        N, T, D, H = (64, 128, 256, 256)
        key = jax.random.key(seed)
        k1, k2, k3, k4 = jax.random.split(key, 4)
        x = jax.random.normal(k1, (N, T, D), dtype=jnp.float32)
        h0 = jax.random.normal(k2, (N, H), dtype=jnp.float32)
        Wx = jax.random.normal(k3, (D, 4 * H), dtype=jnp.float32) / math.sqrt(D)
        Wh = jax.random.normal(k4, (H, 4 * H), dtype=jnp.float32) / math.sqrt(H)
        b = jnp.zeros((4 * H,), dtype=jnp.float32)
        return {'x': x, 'h0': h0, 'Wx': Wx, 'Wh': Wh, 'b': b}
    _L0_cond_all = _L0_cond_setup()
    _L0_cond_in = {k: v for k, v in _L0_cond_all.items() if k in ('Wx', 'Wh', 'b')}
    del _L0_cond_all

    def _L1_cond_setup():
        import jax, jax.numpy as jnp
        import numpy as np
        D_MODEL = 256
        D_FF = 1024
        N_EXPERTS = 8
        TOP_K = 2
        N_SHARED = 2
        B, T = (4, 512)
        key = jax.random.key(seed)
        ks = jax.random.split(key, 9)
        Hs = D_FF // 2
        Hr = D_FF // 4
        inp = {'x': jax.random.normal(ks[0], (B, T, D_MODEL), dtype=jnp.float32), 't_emb': jax.random.normal(ks[1], (B, D_MODEL), dtype=jnp.float32), 'W_router': 0.01 * jax.random.normal(ks[2], (N_EXPERTS, 2 * D_MODEL), dtype=jnp.float32), 'router_bias': jnp.zeros((N_EXPERTS,), dtype=jnp.float32), 's_w1': 0.02 * jax.random.normal(ks[3], (N_SHARED, Hs, D_MODEL), dtype=jnp.float32), 's_w3': 0.02 * jax.random.normal(ks[4], (N_SHARED, Hs, D_MODEL), dtype=jnp.float32), 's_w2': 0.02 * jax.random.normal(ks[5], (N_SHARED, D_MODEL, Hs), dtype=jnp.float32), 'r_w1': 0.02 * jax.random.normal(ks[6], (N_EXPERTS, Hr, D_MODEL), dtype=jnp.float32), 'r_w2': 0.02 * jax.random.normal(ks[7], (N_EXPERTS, D_MODEL, Hr), dtype=jnp.float32)}
        return inp
    _L1_cond_all = _L1_cond_setup()
    _L1_cond_in = {k: v for k, v in _L1_cond_all.items() if k in ('W_router', 'router_bias', 's_w1', 's_w3', 's_w2', 'r_w1', 'r_w2')}
    del _L1_cond_all
    return {'x': x, 'cond_1024': cond_1024, 'L0_cond_Wx': _L0_cond_in['Wx'], 'L0_cond_Wh': _L0_cond_in['Wh'], 'L0_cond_b': _L0_cond_in['b'], 'L1_cond_W_router': _L1_cond_in['W_router'], 'L1_cond_router_bias': _L1_cond_in['router_bias'], 'L1_cond_s_w1': _L1_cond_in['s_w1'], 'L1_cond_s_w3': _L1_cond_in['s_w3'], 'L1_cond_s_w2': _L1_cond_in['s_w2'], 'L1_cond_r_w1': _L1_cond_in['r_w1'], 'L1_cond_r_w2': _L1_cond_in['r_w2']}

def reference(x, cond_1024, L0_cond_Wx, L0_cond_Wh, L0_cond_b, L1_cond_W_router, L1_cond_router_bias, L1_cond_s_w1, L1_cond_s_w3, L1_cond_s_w2, L1_cond_r_w1, L1_cond_r_w2):
    import jax
    import jax.numpy as jnp

    def _L0_cond_ref(x, h0, Wx, Wh, b):
        import jax, jax.numpy as jnp
        import numpy as np
        import math
        N, T, D, H = (64, 128, 256, 256)
        Hdim = h0.shape[1]
        c0 = jnp.zeros_like(h0)
        xW = jnp.einsum('ntd,dk->tnk', x, Wx) + b

        def step(carry, xw_t):
            prev_h, prev_c = carry
            a = xw_t + prev_h @ Wh
            i = jax.nn.sigmoid(a[:, :Hdim])
            f = jax.nn.sigmoid(a[:, Hdim:2 * Hdim])
            o = jax.nn.sigmoid(a[:, 2 * Hdim:3 * Hdim])
            g = jnp.tanh(a[:, 3 * Hdim:])
            next_c = f * prev_c + i * g
            next_h = o * jnp.tanh(next_c)
            return ((next_h, next_c), next_h)
        _, hs = jax.lax.scan(step, (h0, c0), xW)
        return jnp.transpose(hs, (1, 0, 2))

    def _L1_cond_ref(x, t_emb, W_router, router_bias, s_w1, s_w3, s_w2, r_w1, r_w2):
        import jax, jax.numpy as jnp
        import numpy as np
        D_MODEL = 256
        D_FF = 1024
        N_EXPERTS = 8
        TOP_K = 2
        N_SHARED = 2
        B, T = (4, 512)
        Bn, Tn, C = x.shape
        N = Bn * Tn
        x_flat = x.reshape(N, C)
        t_flat = jnp.broadcast_to(t_emb[:, None, :], (Bn, Tn, C)).reshape(N, C)
        shared_out = jnp.zeros_like(x_flat)
        for e in range(N_SHARED):
            h = jax.nn.silu(x_flat @ s_w1[e].T) * (x_flat @ s_w3[e].T)
            shared_out = shared_out + h @ s_w2[e].T
        shared_out = shared_out / N_SHARED
        router_in = jnp.concatenate([x_flat, t_flat], axis=-1)
        s = jax.nn.sigmoid((router_in @ W_router.T).astype(jnp.float32))
        sel_scores = s + router_bias
        _, topk_idx = jax.lax.top_k(sel_scores, TOP_K)
        s_sel = jnp.take_along_axis(s, topk_idx, axis=1)
        denom = jnp.sum(s_sel, axis=1, keepdims=True)
        gates = jnp.where(denom > 1e-09, s_sel / (denom + 1e-09), 1.0 / TOP_K).astype(x.dtype)
        gates_full = jnp.sum(jax.nn.one_hot(topk_idx, N_EXPERTS, dtype=x.dtype) * gates[..., None], axis=1)
        routed_out = jnp.zeros_like(x_flat)
        for e in range(N_EXPERTS):
            h = jax.nn.gelu(x_flat @ r_w1[e].T, approximate=False)
            routed_out = routed_out + h @ r_w2[e].T * gates_full[:, e:e + 1]
        out = (shared_out + routed_out) / (N_SHARED + TOP_K)
        return out.reshape(Bn, Tn, C)
    x = x + _L0_cond_ref(x, cond_1024, L0_cond_Wx, L0_cond_Wh, L0_cond_b)
    x = x + _L1_cond_ref(x, cond_1024, L1_cond_W_router, L1_cond_router_bias, L1_cond_s_w1, L1_cond_s_w3, L1_cond_s_w2, L1_cond_r_w1, L1_cond_r_w2)
    return x

_drawn_inputs = setup_inputs


def setup_inputs(seed=0):
    import zlib

    import numpy as np

    out = dict(_drawn_inputs(seed))
    spreads = {'L0_cond_b': (0.0, 0.1), 'L1_cond_router_bias': (0.0, 0.737)}
    factors = {'cond_1024': 8.0,
     'L1_cond_W_router': 8.0,
     'L1_cond_s_w1': 8.0,
     'L1_cond_s_w3': 8.0,
     'L1_cond_s_w2': 8.0,
     'L1_cond_r_w1': 5.933,
     'L1_cond_r_w2': 5.759}
    for name, (base, spread) in spreads.items():
        noise = np.random.default_rng([zlib.crc32(name.encode()), seed]).standard_normal(out[name].shape)
        drawn = base * np.exp(spread * noise) if base else spread * noise
        out[name] = jnp.asarray(drawn.astype(out[name].dtype))
    for name, factor in factors.items():
        out[name] = (out[name] * factor).astype(out[name].dtype)
    return out
```

```python
from contextlib import ExitStack

import numpy as np

import concourse.bass as bass
from concourse import mybir

ALU = mybir.AluOpType
ACT = mybir.ActivationFunctionType
F32 = mybir.dt.float32
F16 = mybir.dt.float16
U32 = mybir.dt.uint32
AX = mybir.AxisListType
RMAX = bass.bass_isa.ReduceOp.max

P = 128
B, T, D = 2, 1024, 256
KC = D // P
H4 = 4 * D
MC = H4 // P
HC = KC * B
GATES = MC * B
GI, FG, OG = 4 * B, 2 * B, 2 * B
NTOK = B * T
U = 8
BANK = 512
TILE = 512
NT = NTOK // TILE
SUB = TILE // P
NE = 8
FSH = 1024
NQ = FSH // P
HR = 256
S0 = 2.0 ** 20
OWN = 5


def cond_resid_kernel(nc, xT, condT, wx, wh, bT, wr, rb, sw1, sw3, sw2, rw1, rw2, eye, iota, outT):
    with ExitStack() as ctx:
        def sb(name, shape, dt=F32):
            return ctx.enter_context(nc.sbuf_tensor(name, shape, dt))

        def sem(name):
            return ctx.enter_context(nc.semaphore(name))

        gates = ctx.enter_context(nc.psum_tensor("gates", [P, 3 * BANK], F32))
        work = ctx.enter_context(nc.psum_tensor("work", [P, 5 * BANK], F32))
        gi_ps = gates[:, BANK - GI:BANK]
        f_ps = gates[:, BANK:BANK + FG]
        o_ps = gates[:, 2 * BANK:2 * BANK + OG]
        pairs = [gates[:, BANK:3 * BANK], work[:, 0:2 * BANK]]
        acc = work[:, 2 * BANK:4 * BANK]
        gb_ps = work[:, 4 * BANK:5 * BANK]

        x_sb = sb("x_sb", [P, KC, NTOK])
        cond_sb = sb("cond_sb", [P, HC])
        wx_sb = sb("wx_sb", [P, KC, H4])
        wh_sb = sb("wh_sb", [P, KC, H4])
        wh_hi = sb("wh_hi", [P, KC, H4], F16)
        wh_lo = sb("wh_lo", [P, KC, H4], F16)
        b_sb = sb("b_sb", [P, MC])
        xw = sb("xw", [P, (T + 1) * GATES])
        wr_sb = sb("wr_sb", [P, 2 * KC, NE])
        rb_sb = sb("rb_sb", [P, NE])
        sw1_sb = sb("sw1_sb", [P, KC, FSH])
        sw3_sb = sb("sw3_sb", [P, KC, FSH])
        sw2_sb = sb("sw2_sb", [P, NQ, D])
        rw1_sb = sb("rw1_sb", [P, KC, NE * HR])
        rw2_sb = sb("rw2_sb", [P, NE * HR // P, D])
        eye_sb = sb("eye_sb", [P, P])
        iota_sb = sb("iota_sb", [P, NE])

        wmax = sb("wmax", [P, 1])
        wtop = sb("wtop", [P, 1])
        sc = sb("sc", [P, 8])
        half_p, inv_p, w_scale = sc[:, 0:1], sc[:, 1:2], sc[:, 2:3]
        zero16 = sb("zero16", [P, P], F16)
        h_hi = sb("h_hi", [P, HC], F16)
        h_lo = sb("h_lo", [P, HC], F16)
        h32 = sb("h32", [P, U, HC])
        tgi = sb("tgi", [P, GI])
        tf = sb("tf", [P, FG, 2])
        to = sb("to", [P, OG])
        to1 = sb("to1", [P, OG])
        ig2 = sb("ig2", [P, HC])
        add = sb("add", [P, HC, 2])
        cs = sb("cs", [P, HC, 2])
        tc = sb("tc", [P, HC])

        cexp = sb("cexp", [P, KC, P])
        tpart = sb("tpart", [P, NE])
        xt = sb("xt", [P, KC, TILE])
        rt = sb("rt", [P, 10, SUB, NE])
        m8 = sb("m8", [P, SUB, 8])
        i8 = sb("i8", [P, SUB, 8], U32)
        if8 = sb("if8", [P, SUB, 8])
        den = sb("den", [P, 4, SUB])
        gfull = sb("gfull", [P, SUB, NE])
        th = sb("th", [P, 2, 2 * TILE])
        uu = sb("uu", [P, 2, TILE])
        hid = sb("hid", [P, 2, 2 * TILE])
        osb = sb("osb", [P, KC, TILE])

        s_x, s_lw, s_mw = sem("x_loaded"), sem("lstm_weights_loaded"), sem("moe_weights_loaded")
        s_own = sem("vector_step_done")
        s_setup = sem("vector_setup_done")
        s_top = sem("max_over_partitions")
        s_bits = sem("psum_bits_set")
        s_xwp, s_xwc = sem("xw_product"), sem("xw_copied")
        s_hhi, s_hlo = sem("h_hi_ready"), sem("h_lo_ready")
        s_gi, s_f, s_o = sem("gi_summed"), sem("f_summed"), sem("o_summed")
        s_tgi, s_tf, s_to, s_tc = sem("gi_tanh"), sem("f_tanh"), sem("o_tanh"), sem("c_tanh")
        s_c = sem("c_ready")
        s_seq = sem("lstm_done")
        s_xt = sem("tile_copied")
        s_lg, s_lc, s_lt = sem("logits"), sem("logits_clamped"), sem("logits_tanh")
        s_chain = sem("vector_router_done")
        s_gate = sem("gates_ready")
        s_up, s_act, s_hid, s_dn = sem("up_done"), sem("act_done"), sem("hidden_ready"), sem("down_done")
        s_gb, s_acc = sem("gate_broadcast"), sem("tile_summed")
        s_fin, s_st = sem("tile_finished"), sem("tile_stored")

        def take_back(eng, s, n):
            eng.wait_ge(s, n)
            eng.sem_inc(s, -n)

        block = ctx.enter_context(nc.Block())

        @block.sync
        def _(sp):
            for dst, src in ((x_sb, xT), (wx_sb, wx), (b_sb, bT)):
                sp.dma_start(dst[:], src).then_inc(s_x, 16)
            for dst, src in ((wh_sb, wh), (cond_sb, condT)):
                sp.dma_start(dst[:], src).then_inc(s_lw, 16)
            for dst, src in ((wr_sb, wr), (rb_sb, rb), (sw1_sb, sw1), (sw3_sb, sw3), (sw2_sb, sw2),
                             (rw1_sb, rw1), (rw2_sb, rw2), (eye_sb, eye), (iota_sb, iota)):
                sp.dma_start(dst[:], src).then_inc(s_mw, 16)
            with sp.Fori(0, NT) as n:
                sp.sem_inc(s_acc, 1)
                take_back(sp, s_fin, 1)
                sp.dma_start(outT[:, :, bass.ds(n * TILE, TILE)], osb[:]).then_inc(s_st, 16)
                sp.wait_ge(s_st, 16)
                sp.sem_inc(s_st, -16)

        @block.gpsimd
        def _(pool):
            pool.wait_ge(s_setup, 1)
            nc.gpsimd.partition_all_reduce(wtop[:], wmax[:], P, RMAX).then_inc(s_top, 1)

        def silu_or_gelu(k):
            return k < NQ

        @block.scalar
        def _(act):
            nc.scalar.preload_act_table(ACT.Gelu)
            with act.Fori(0, T // U):
                for u in range(U):
                    act.wait_ge(s_gi, u + 1)
                    nc.scalar.activation(tgi[:], gi_ps, ACT.Tanh, scale=0.5 / S0).then_inc(s_tgi, 1)
                    act.wait_ge(s_f, u + 1)
                    nc.scalar.activation(tf[:, :, 1], f_ps, ACT.Tanh, scale=0.5 / S0).then_inc(s_tf, 1)
                    act.wait_ge(s_o, u + 1)
                    nc.scalar.activation(to[:], o_ps, ACT.Tanh, scale=0.5 / S0).then_inc(s_to, 1)
                    act.wait_ge(s_c, u + 1)
                    nc.scalar.activation(tc[:], cs[:, :, 1], ACT.Tanh).then_inc(s_tc, 1)
                for s in (s_gi, s_f, s_o, s_c):
                    take_back(act, s, U)
            with act.Fori(0, NT):
                act.wait_ge(s_lc, 1)
                nc.scalar.activation(rt[:, 1, :, :], rt[:, 0, :, :], ACT.Tanh, scale=-1.0 / 64).then_inc(s_lt, 1)
                for k in range(2 * NQ):
                    act.wait_ge(s_up, k + 1)
                    if k < NQ:
                        nc.scalar.activation(th[:, k % 2, 0:TILE], pairs[k % 2][:, 0:TILE], ACT.Tanh, scale=0.5).then_inc(s_act, 1)
                    else:
                        nc.scalar.activation(th[:, k % 2, :], pairs[k % 2], ACT.Gelu).then_inc(s_act, 1)
                take_back(act, s_up, 2 * NQ)
                take_back(act, s_lc, 1)

        @block.vector
        def _(dve):
            v = nc.vector
            done = [0]

            def link(ins):
                done[0] += 1
                ins.then_inc(s_own, 1)
                dve.wait_ge(s_own, done[0])

            dve.wait_ge(s_lw, 32)
            v.tensor_reduce(wmax[:], wh_sb[:], AX.XY, ALU.max, apply_absolute_value=True).then_inc(s_setup, 1)
            v.memset(zero16[:], 0.0).then_inc(s_setup, 1)
            dve.wait_ge(s_top, 1)
            link(v.tensor_scalar(sc[:, 3:4], wtop[:], 2.0 ** -40, None, ALU.max))
            link(v.tensor_scalar(sc[:, 4:5].bitcast(U32), sc[:, 3:4].bitcast(U32), 0x7F800000, None, ALU.bitwise_and))
            link(v.reciprocal(sc[:, 5:6], sc[:, 4:5]))
            link(v.tensor_scalar(sc[:, 6:7], sc[:, 5:6], 2.0 ** 13, S0, ALU.mult, ALU.min))
            link(v.tensor_scalar(w_scale, sc[:, 6:7], S0 / 2.0 ** 15, None, ALU.max))
            link(v.tensor_scalar(inv_p, w_scale, 1.0 / S0, None, ALU.mult))
            link(v.reciprocal(sc[:, 7:8], inv_p))
            link(v.tensor_scalar(half_p, sc[:, 7:8], 0.5, None, ALU.mult))
            for lo, hi, more in ((0, D, 2.0), (D, H4, 1.0)):
                link(v.tensor_scalar(wh_hi[:, :, lo:hi], wh_sb[:, :, lo:hi], w_scale, more, ALU.mult, ALU.mult))
                link(v.tensor_scalar(xw[:, 0:KC * (hi - lo)].rearrange("p (k n) -> p k n", k=KC), wh_sb[:, :, lo:hi],
                                     w_scale, more, ALU.mult, ALU.mult))
                link(v.tensor_tensor(wh_lo[:, :, lo:hi], xw[:, 0:KC * (hi - lo)].rearrange("p (k n) -> p k n", k=KC),
                                     wh_hi[:, :, lo:hi], ALU.subtract))
            dve.wait_ge(s_x, 48)
            steps = TILE // B
            for n in range(NT):
                for m in range(MC):
                    k = n * MC + m
                    dst = xw[:, n * steps * GATES:(n + 1) * steps * GATES].rearrange("p (t g) -> p t g", g=GATES)
                    dve.wait_ge(s_xwp, k + 1)
                    ins = v.tensor_scalar(dst[:, :, m * B:(m + 1) * B],
                                          work[:, (k % 2) * BANK:(k % 2) * BANK + TILE].rearrange("p (t b) -> p t b", b=B),
                                          b_sb[:, m:m + 1], S0 * (2.0 if m < 2 else 1.0), ALU.add, ALU.mult)
                    ins.then_inc(s_xwc, 1)
            v.memset(xw[:, T * GATES:(T + 1) * GATES], 0.0).then_inc(s_xwc, 1)
            dve.wait_ge(s_xwp, NT * MC + 1)
            dve.wait_ge(s_xwc, NT * MC + 1)
            link(v.tensor_scalar(rt[:, 0, 0:2, :], work[:, 2 * BANK:2 * BANK + GATES], S0, None, ALU.mult))
            link(v.tensor_scalar(rt[:, 0, 0, 0:4], rt[:, 0, 0, 0:4], 2.0, None, ALU.mult))
            link(v.tensor_tensor(xw[:, 0:GATES], xw[:, 0:GATES], rt[:, 0, 0:2, :], ALU.add))
            dve.wait_ge(s_bits, 1)
            v.tensor_copy(gates[:, BANK - GI:BANK + FG], xw[:, 0:GI + FG])
            v.tensor_copy(o_ps, xw[:, GI + FG:GATES])
            link(v.memset(tf[:], 0.0))
            link(v.memset(add[:], 0.0))
            v.memset(h_hi[:], 0.0).then_inc(s_hhi, 1)
            v.memset(h_lo[:], 0.0).then_inc(s_hlo, 1)
            take_back(dve, s_own, done[0])

            with dve.Fori(0, T // U) as it:
                for u in range(U):
                    own = OWN * u
                    dve.wait_ge(s_tgi, u + 1)
                    v.scalar_tensor_tensor(ig2[:], tgi[:, HC:2 * HC], 1.0, tgi[:, 0:HC], ALU.add, ALU.mult).then_inc(s_own, 1)
                    dve.wait_ge(s_own, own + 1)
                    v.scalar_tensor_tensor(add[:, :, 1], ig2[:], 0.5, add[:, :, 0], ALU.mult, ALU.add).then_inc(s_own, 1)
                    dve.wait_ge(s_tf, u + 1)
                    dve.wait_ge(s_own, own + 2)
                    v.tensor_tensor_scan(cs[:].rearrange("p c two -> p (c two)"), tf[:].rearrange("p c two -> p (c two)"),
                                         add[:].rearrange("p c two -> p (c two)"), 0.0, ALU.mult, ALU.add).then_inc(s_c, 1)
                    dve.wait_ge(s_to, u + 1)
                    v.tensor_scalar(to1[:], to[:], 1.0, half_p, ALU.add, ALU.mult).then_inc(s_own, 1)
                    nxt = (it * U + u + 1) * GATES
                    v.tensor_copy(gates[:, BANK - GI:BANK + FG], xw[:, bass.ds(nxt, GI + FG)])
                    v.tensor_copy(o_ps, xw[:, bass.ds(nxt + GI + FG, OG)])
                    dve.wait_ge(s_tc, u + 1)
                    dve.wait_ge(s_own, own + 3)
                    v.tensor_tensor(h_hi[:], to1[:], tc[:], ALU.mult).then_inc(s_hhi, 1)
                    v.tensor_tensor(h32[:, u, :], to1[:], tc[:], ALU.mult).then_inc(s_own, 1)
                    dve.wait_ge(s_own, own + 4)
                    v.tensor_tensor(h_lo[:], h32[:, u, :], h_hi[:], ALU.subtract).then_inc(s_hlo, 1)
                    v.tensor_scalar(add[:, :, 0], cs[:, :, 1], 0.5, None, ALU.mult).then_inc(s_own, 1)
                for k in range(KC):
                    xs = x_sb[:, k, bass.ds(it * (U * B), U * B)].rearrange("p (u b) -> p u b", b=B)
                    v.scalar_tensor_tensor(xs, h32[:, :, k * B:(k + 1) * B], inv_p, xs, ALU.mult, ALU.add).then_inc(s_own, 1)
                for s in (s_tgi, s_tf, s_to, s_tc):
                    take_back(dve, s, U)
                take_back(dve, s_own, OWN * U + KC)

            dve.wait_ge(s_mw, 16 * 9)
            v.tensor_copy(cexp[:].rearrange("p k (t b) -> p k t b", b=B),
                          cond_sb[:].rearrange("p (k o b) -> p k o b", k=KC, o=1).broadcast_to([P, KC, P // B, B])).then_inc(s_seq, 1)
            dve.wait_ge(s_lg, 1)
            v.tensor_copy(tpart[:], gb_ps[:, 0:NE]).then_inc(s_chain, 1)
            take_back(dve, s_chain, 1)
            take_back(dve, s_lg, 1)

            with dve.Fori(0, NT) as n:
                ch = [0]

                def chain(ins):
                    ch[0] += 1
                    ins.then_inc(s_chain, 1)
                    dve.wait_ge(s_chain, ch[0])

                v.tensor_copy(xt[:], x_sb[:, :, bass.ds(n * TILE, TILE)]).then_inc(s_xt, 1)
                dve.wait_ge(s_lg, 1)
                lg, nl, e, num, dn, s, mask, t0, t1, t2 = (rt[:, j] for j in range(10))
                chain(v.tensor_tensor(t0, gb_ps[:, 0:SUB * NE].rearrange("p (s e) -> p s e", e=NE),
                                      tpart[:].rearrange("p (o e) -> p o e", o=1).broadcast_to([P, SUB, NE]), ALU.add))
                v.tensor_scalar(lg, t0, 80.0, -80.0, ALU.min, ALU.max).then_inc(s_lc, 1)
                dve.wait_ge(s_lt, 1)
                chain(v.tensor_scalar(num, nl, 1.0, None, ALU.add))
                chain(v.tensor_scalar(dn, nl, -1.0, 1.0, ALU.mult, ALU.add))
                chain(v.reciprocal(t0, dn))
                chain(v.tensor_tensor(e, num, t0, ALU.mult))
                for a, b in ((t0, e), (e, t0), (t0, e), (e, t0), (t0, e)):
                    chain(v.tensor_tensor(a, b, b, ALU.mult))
                chain(v.tensor_scalar(t1, t0, 1.0, None, ALU.add))
                chain(v.reciprocal(s, t1))
                chain(v.tensor_tensor(t0, s, rb_sb[:].rearrange("p (o e) -> p o e", o=1).broadcast_to([P, SUB, NE]), ALU.add))
                for j in range(SUB):
                    ins = v.max(m8[:, j, :], t0[:, j, :])
                    ins.then_inc(s_chain, 1)
                    ch[0] += 1
                dve.wait_ge(s_chain, ch[0])
                for j in range(SUB):
                    v.max_index(i8[:, j, :], m8[:, j, :], t0[:, j, :]).then_inc(s_chain, 1)
                    ch[0] += 1
                dve.wait_ge(s_chain, ch[0])
                chain(v.tensor_copy(if8[:], i8[:]))
                for j in range(SUB):
                    v.tensor_scalar(t1[:, j, :], iota_sb[:], if8[:, j, 0:1], None, ALU.is_equal).then_inc(s_chain, 1)
                    ch[0] += 1
                dve.wait_ge(s_chain, ch[0])
                for j in range(SUB):
                    v.scalar_tensor_tensor(mask[:, j, :], iota_sb[:], if8[:, j, 1:2], t1[:, j, :],
                                           ALU.is_equal, ALU.add).then_inc(s_chain, 1)
                    ch[0] += 1
                dve.wait_ge(s_chain, ch[0])
                chain(v.tensor_tensor(t0, s, mask, ALU.mult))
                chain(v.tensor_reduce(den[:, 0, :], t0, AX.X, ALU.add))
                chain(v.tensor_scalar(den[:, 1, :], den[:, 0, :], 1e-9, None, ALU.add))
                chain(v.reciprocal(den[:, 2, :], den[:, 1, :]))
                chain(v.tensor_scalar(den[:, 3, :], den[:, 0, :], 1e-9, None, ALU.is_gt))
                chain(v.tensor_tensor(den[:, 2, :], den[:, 2, :], den[:, 3, :], ALU.mult))
                chain(v.tensor_scalar(den[:, 1, :], den[:, 0, :], 1e-9, 0.5, ALU.is_le, ALU.mult))
                for j in range(SUB):
                    v.tensor_scalar(t1[:, j, :], mask[:, j, :], den[:, 1, j:j + 1], None, ALU.mult).then_inc(s_chain, 1)
                    ch[0] += 1
                dve.wait_ge(s_chain, ch[0])
                for j in range(SUB):
                    v.scalar_tensor_tensor(gfull[:, j, :], t0[:, j, :], den[:, 2, j:j + 1], t1[:, j, :],
                                           ALU.mult, ALU.add).then_inc(s_chain, 1)
                    ch[0] += 1
                dve.wait_ge(s_chain, ch[0])
                v.tensor_copy(gfull[:], gfull[:]).then_inc(s_gate, 1)
                for k in range(2 * NQ):
                    dve.wait_ge(s_act, k + 1)
                    if k >= 2:
                        dve.wait_ge(s_dn, k - 1)
                    if k < NQ:
                        chain(v.scalar_tensor_tensor(uu[:, k % 2, :], th[:, k % 2, 0:TILE], 1.0, pairs[k % 2][:, 0:TILE],
                                                     ALU.add, ALU.mult))
                        v.scalar_tensor_tensor(hid[:, k % 2, 0:TILE], uu[:, k % 2, :], 1.0 / 16, pairs[k % 2][:, TILE:2 * TILE],
                                               ALU.mult, ALU.mult).then_inc(s_hid, 1)
                    else:
                        dve.wait_ge(s_gb, k - NQ + 1)
                        gbc = gb_ps.rearrange("p (o t) -> p o t", o=1).broadcast_to([P, 2, TILE])
                        v.scalar_tensor_tensor(hid[:, k % 2, :].rearrange("p (o t) -> p o t", o=2),
                                               th[:, k % 2, :].rearrange("p (o t) -> p o t", o=2), 0.25, gbc,
                                               ALU.mult, ALU.mult).then_inc(s_hid, 1)
                dve.wait_ge(s_dn, 2 * NQ)
                take_back(dve, s_acc, 1)
                v.tensor_tensor(osb[:], acc.rearrange("p (k t) -> p k t", k=KC),
                                x_sb[:, :, bass.ds(n * TILE, TILE)], ALU.add).then_inc(s_fin, 1)
                take_back(dve, s_chain, ch[0])
                take_back(dve, s_lg, 1)
                take_back(dve, s_act, 2 * NQ)
                take_back(dve, s_dn, 2 * NQ)
                take_back(dve, s_gb, NE)
                take_back(dve, s_lt, 1)

        @block.tensor
        def _(pe):
            mm = nc.tensor.matmul
            pe.wait_ge(s_setup, 2)
            for ps, n in ((gi_ps, GI), (f_ps, FG), (o_ps, OG)):
                last = mm(ps, zero16[:], zero16[:, 0:n], start=True, stop=True, skip_group_check=True)
            last.then_inc(s_bits, 1)
            pe.wait_ge(s_x, 48)
            for n in range(NT):
                for m in range(MC):
                    k = n * MC + m
                    if k >= 2:
                        pe.wait_ge(s_xwc, k - 1)
                    for c in range(KC):
                        last = mm(work[:, (k % 2) * BANK:(k % 2) * BANK + TILE], wx_sb[:, c, m * P:(m + 1) * P],
                                  x_sb[:, c, n * TILE:(n + 1) * TILE], start=(c == 0), stop=(c == KC - 1))
                    last.then_inc(s_xwp, 1)
            pe.wait_ge(s_lw, 32)
            for m in range(MC):
                for c in range(KC):
                    last = mm(work[:, 2 * BANK + m * B:2 * BANK + (m + 1) * B], wh_sb[:, c, m * P:(m + 1) * P],
                              cond_sb[:, c * B:(c + 1) * B], start=(c == 0), stop=(c == KC - 1))
            last.then_inc(s_xwp, 1)

            def gate(ps, m0, n, halves):
                for j in range(n):
                    m = m0 + j
                    for c in range(KC):
                        for w, h in halves:
                            last = mm(ps[:, j * B:(j + 1) * B], w[:, c, m * P:(m + 1) * P], h[:, c * B:(c + 1) * B],
                                      start=False, stop=True, skip_group_check=True)
                return last

            with pe.Fori(0, T // U):
                for u in range(U):
                    pe.wait_ge(s_hhi, u + 1)
                    gate(gi_ps, 0, 4, ((wh_lo, h_hi), (wh_hi, h_hi)))
                    pe.wait_ge(s_hlo, u + 1)
                    gate(gi_ps, 0, 4, ((wh_hi, h_lo),)).then_inc(s_gi, 1)
                    gate(f_ps, 4, 2, ((wh_lo, h_hi), (wh_hi, h_hi), (wh_hi, h_lo))).then_inc(s_f, 1)
                    gate(o_ps, 6, 2, ((wh_lo, h_hi), (wh_hi, h_hi), (wh_hi, h_lo))).then_inc(s_o, 1)
                take_back(pe, s_hhi, U)
                take_back(pe, s_hlo, U)

            pe.wait_ge(s_seq, 1)
            pe.wait_ge(s_mw, 16 * 9)
            for c in range(KC):
                last = mm(gb_ps[:, 0:NE], cexp[:, c, :], wr_sb[:, KC + c, :], start=(c == 0), stop=(c == KC - 1))
            last.then_inc(s_lg, 1)

            def up(k):
                if k >= 2:
                    pe.wait_ge(s_hid, k - 1)
                for half in range(2):
                    w, at = ((sw1_sb if half == 0 else sw3_sb), k * P) if k < NQ else (rw1_sb, (k - NQ) * HR + half * P)
                    for c in range(KC):
                        last = mm(pairs[k % 2][:, half * TILE:(half + 1) * TILE], w[:, c, at:at + P], xt[:, c, :],
                                  start=(c == 0), stop=(c == KC - 1))
                last.then_inc(s_up, 1)

            def spread(e):
                pe.wait_ge(s_hid, NQ + e)
                for j in range(SUB):
                    last = mm(gb_ps[:, j * P:(j + 1) * P], gfull[:, j, e:e + 1].broadcast_to([P, P]), eye_sb[:],
                              start=True, stop=True)
                last.then_inc(s_gb, 1)

            def down(k):
                pe.wait_ge(s_hid, k + 1)
                halves = 1 if k < NQ else 2
                for half in range(halves):
                    w = sw2_sb[:, k, :] if k < NQ else rw2_sb[:, (k - NQ) * 2 + half, :]
                    for c in range(KC):
                        last = mm(acc[:, c * TILE:(c + 1) * TILE], w[:, c * P:(c + 1) * P],
                                  hid[:, k % 2, half * TILE:(half + 1) * TILE], start=(k == 0), stop=(k == 2 * NQ - 1 and half == 1),
                                  skip_group_check=True)
                last.then_inc(s_dn, 1)

            with pe.Fori(0, NT):
                pe.wait_ge(s_xt, 1)
                for j in range(SUB):
                    for c in range(KC):
                        last = mm(gb_ps[:, j * NE:(j + 1) * NE], xt[:, c, j * P:(j + 1) * P], wr_sb[:, c, :],
                                  start=(c == 0), stop=(c == KC - 1))
                last.then_inc(s_lg, 1)
                up(0)
                for k in range(1, 2 * NQ):
                    up(k)
                    if k == NQ:
                        pe.wait_ge(s_gate, 1)
                    if k >= NQ:
                        spread(k - NQ)
                    down(k - 1)
                down(2 * NQ - 1)
                take_back(pe, s_xt, 1)
                take_back(pe, s_hid, 2 * NQ)
                take_back(pe, s_gate, 1)


def kernel(x, cond_1024, L0_cond_Wx, L0_cond_Wh, L0_cond_b, L1_cond_W_router, L1_cond_router_bias,
           L1_cond_s_w1, L1_cond_s_w3, L1_cond_s_w2, L1_cond_r_w1, L1_cond_r_w2):
    import concourse.bacc as bacc
    from concourse.bass_utils import run_bass_kernel_spmd

    def rows(a):
        a = np.asarray(a)
        return np.ascontiguousarray(a.reshape(a.shape[0] // P, P, -1).transpose(1, 0, 2))

    def gate_order(a):
        a = np.asarray(a)
        return np.concatenate([a[..., 3 * D:], a[..., :3 * D]], axis=-1)

    s_w1, s_w3, s_w2, r_w1, r_w2 = (np.asarray(a) for a in (L1_cond_s_w1, L1_cond_s_w3, L1_cond_s_w2, L1_cond_r_w1, L1_cond_r_w2))
    arrays = {
        "xT": rows(np.asarray(x).transpose(2, 1, 0).reshape(D, NTOK)),
        "condT": rows(np.asarray(cond_1024).T).reshape(P, HC),
        "wx": rows(gate_order(L0_cond_Wx)),
        "wh": rows(gate_order(L0_cond_Wh)),
        "bT": np.ascontiguousarray(gate_order(L0_cond_b).reshape(MC, P).T),
        "wr": rows(np.asarray(L1_cond_W_router).T),
        "rb": np.ascontiguousarray(np.broadcast_to(np.asarray(L1_cond_router_bias), (P, NE))),
        "sw1": rows(s_w1.reshape(FSH, D).T),
        "sw3": rows(s_w3.reshape(FSH, D).T),
        "sw2": rows(s_w2.transpose(0, 2, 1).reshape(FSH, D)),
        "rw1": rows(r_w1.reshape(NE * HR, D).T),
        "rw2": rows(r_w2.transpose(0, 2, 1).reshape(NE * HR, D)),
        "eye": np.eye(P, dtype=np.float32),
        "iota": np.ascontiguousarray(np.broadcast_to(np.arange(NE, dtype=np.float32), (P, NE))),
    }
    nc = bacc.Bacc("TRN2", target_bir_lowering=False, num_devices=1)
    args = [nc.dram_tensor(n, a.shape, mybir.dt.from_np(a.dtype), kind="ExternalInput").ap() for n, a in arrays.items()]
    args.append(nc.dram_tensor("outT", (P, KC, NTOK), F32, kind="ExternalOutput").ap())
    cond_resid_kernel(nc, *args)
    r = run_bass_kernel_spmd(nc, [arrays], core_ids=[0])
    got = r.results[0]["outT"]
    return np.ascontiguousarray(got.transpose(1, 0, 2).reshape(D, T, B).transpose(2, 1, 0))
```

```python
from contextlib import ExitStack

import numpy as np

import concourse.bass as bass
from concourse import mybir

ALU = mybir.AluOpType
ACT = mybir.ActivationFunctionType
F32 = mybir.dt.float32
F16 = mybir.dt.float16
U32 = mybir.dt.uint32
AX = mybir.AxisListType
RMAX = bass.bass_isa.ReduceOp.max

P = 128
B, T, D = 2, 1024, 256
KC = D // P
H4 = 4 * D
MC = H4 // P
HC = KC * B
GATES = MC * B
GI, FG, OG = 4 * B, 2 * B, 2 * B
PARTS = 3
NTOK = B * T
BANK = 512
TS = 64
TT = TS * B
NT = T // TS
HS = 8
PIECES = TS // HS
NE = 8
FSH = 1024
NQ = FSH // P
HR = 256
RC = HR // P
S0 = 2.0 ** 20
F_OF, GI_OF, O_OF, C_OF = 1, 2, 3, 4
LOGITS = 1
LT = 3
UP1 = {3 * q + 2: q for q in range(NQ)}
UP3 = {3 * q + 3: q for q in range(NQ)}
DOWN_SH = {3 * q + 4: q for q in range(NQ)}
R0 = 3 * NQ + 2
UP_R0 = {R0 + 4 * e: e for e in range(NE)}
UP_R1 = {R0 + 4 * e + 1: e for e in range(NE)}
GATE0 = {R0 + 4 * e + 2: e for e in range(NE)}
GATE1 = {R0 + 4 * e + 3: e for e in range(NE)}
DOWN_R0 = {R0 + 4 * e + 6: e for e in range(NE)}
DOWN_R1 = {R0 + 4 * e + 7: e for e in range(NE)}
LAST = R0 + 4 * NE + 3


def cond_resid_kernel(nc, xT, condT, wx, wh, bT, wr, rb, sw1, sw3, sw2, rw1, rw2, eye, iota, outT):
    with ExitStack() as ctx:
        def sb(name, shape, dt=F32):
            return ctx.enter_context(nc.sbuf_tensor(name, shape, dt))

        def sem(name):
            return ctx.enter_context(nc.semaphore(name))

        def bank(name, n=1):
            return ctx.enter_context(nc.psum_tensor(name, [P, n * BANK], F32))

        gates = bank("gates", 3)
        state, up_sh, up_rt, acc_lg, xw_gb = (bank(n) for n in ("state", "up_sh", "up_rt", "acc_lg", "xw_gb"))
        gi_ps = gates[:, BANK - PARTS * GI:BANK]
        f_ps = gates[:, BANK:BANK + PARTS * FG]
        o_ps = gates[:, 2 * BANK:2 * BANK + PARTS * OG]
        gif_xw = gates[:, BANK - PARTS * GI:BANK + PARTS * FG].rearrange("p (m j b) -> p m j b", j=PARTS, b=B)[:, :, 2, :]
        o_xw = o_ps.rearrange("p (m j b) -> p m j b", j=PARTS, b=B)[:, :, 2, :]
        gi_sum = gates[:, 0:GI]
        f_sum = gates[:, 2 * BANK - FG:2 * BANK]
        o_sum = gates[:, 3 * BANK - OG:3 * BANK]
        cs = state[:, 0:HC * 3].rearrange("p (c j) -> p c j", j=3)
        a1, a3 = up_sh[:, 0:TT], up_rt[:, 0:TT]
        acc = acc_lg[:, 0:KC * TT]
        logits = acc_lg[:, KC * TT:KC * TT + NE]
        xw_ps, gb_ps = xw_gb[:, 0:TT], xw_gb[:, TT:2 * TT]

        x_sb = sb("x_sb", [P, KC, NTOK + TT])
        xw = sb("xw", [P, (T + TS) * GATES])
        cond_sb = sb("cond_sb", [P, HC])
        wx_sb = sb("wx_sb", [P, KC, H4])
        wh_sb = sb("wh_sb", [P, KC, H4])
        wh_hi = sb("wh_hi", [P, KC, H4], F16)
        wh_lo = sb("wh_lo", [P, KC, H4], F16)
        b_sb = sb("b_sb", [P, MC])
        b_scaled = sb("b_scaled", [P, MC])
        wr_sb = sb("wr_sb", [P, 2 * KC, NE])
        rb_sb = sb("rb_sb", [P, NE])
        sw1_sb = sb("sw1_sb", [P, KC, FSH])
        sw3_sb = sb("sw3_sb", [P, KC, FSH])
        sw2_sb = sb("sw2_sb", [P, NQ, D])
        rw1_sb = sb("rw1_sb", [P, KC, NE * HR])
        rw2_sb = sb("rw2_sb", [P, NE * RC, D])
        eye_sb = sb("eye_sb", [P, P])
        iota_sb = sb("iota_sb", [P, NE])

        wmax = sb("wmax", [P, 1])
        wtop = sb("wtop", [P, 1])
        sc = sb("sc", [P, 8])
        half_p, inv_p, w_scale = sc[:, 0:1], sc[:, 1:2], sc[:, 2:3]
        half_p4 = sb("half_p4", [P, OG])
        hw0 = sb("hw0", [P, GATES])
        hh = sb("hh", [P, KC, 2, B], F16)
        h32 = sb("h32", [P, 2, HS, HC])
        seeds = sb("seeds", [P, 2, HS, GATES])
        fac_add = sb("fac_add", [P, 2, HC, 3])
        fac, addend = fac_add[:, 0, :, :], fac_add[:, 1, :, :]
        gi_out = fac_add[:].rearrange("p a c j -> p (a c j)")[:, 2:2 + 2 * (HC * 3 - 1)].rearrange(
            "p (a z) -> p a z", a=2)[:, :, 0:HC * 3 - 2:3]
        tf = sb("tf", [P, FG])
        tc = sb("tc", [P, HC])
        c_now = sb("c_now", [P, HC])
        to = sb("to", [P, OG])
        to1 = sb("to1", [P, OG])

        cexp = sb("cexp", [P, KC, TT])
        h_part = sb("h_part", [P, 2, KC, HS * B])
        x_new = sb("x_new", [P, KC, TT])
        xt = sb("xt", [P, KC, TT])
        rt = sb("rt", [P, 10, NE])
        m8 = sb("m8", [P, 8])
        i8 = sb("i8", [P, 8], U32)
        if8 = sb("if8", [P, 8])
        den = sb("den", [P, 6])
        gfull = sb("gfull", [P, NE])
        th = sb("th", [P, TT])
        uu = sb("uu", [P, TT])
        hid_sh = sb("hid_sh", [P, TT])
        ge = sb("ge", [P, RC, TT])
        hid_rt = sb("hid_rt", [P, 2, RC, TT])
        osb = sb("osb", [P, KC, TT])

        s_lw, s_xw0, s_in, s_mw = sem("wh_loaded"), sem("first_x_loaded"), sem("all_x_loaded"), sem("moe_weights_loaded")
        s_link, s_own = sem("vector_setup_step"), sem("vector_step_done")
        s_setup = sem("vector_setup_done")
        s_top = sem("max_over_partitions")
        s_xwp0, s_xwc0 = sem("first_xw_product"), sem("first_xw_copied")
        s_hhi, s_hlo = sem("h_hi_ready"), sem("h_lo_ready")
        s_mul, s_sum, s_tanh = sem("f_gi_o_multiplied"), sem("f_gi_o_c_summed"), sem("f_gi_o_c_tanh")
        s_piece, s_staged, s_added = sem("piece_of_steps_done"), sem("piece_staged"), sem("h_added_to_x")
        s_xt = sem("tile_copied")
        s_xwp, s_xwe = sem("xw_product"), sem("xw_copied")
        s_lg, s_lc, s_lt = sem("logits"), sem("logits_clamped"), sem("logits_tanh")
        s_chain = sem("vector_router_step")
        s_gate = sem("gates_ready")
        s_up, s_up3, s_act = sem("up_for_scalar"), sem("up_w3_done"), sem("activated")
        s_u, s_hs, s_hr = sem("silu_product"), sem("shared_hidden_ready"), sem("routed_hidden_ready")
        s_dn = sem("mixture_summed")
        s_fin, s_st, s_free = sem("tile_finished"), sem("tile_stored"), sem("output_buffer_free")

        def take_back(eng, s, n):
            eng.wait_ge(s, n)
            eng.sem_inc(s, -n)

        block = ctx.enter_context(nc.Block())

        @block.sync
        def _(sp):
            for dst, src in ((wh_sb[:], wh), (cond_sb[:], condT)):
                sp.dma_start(dst, src).then_inc(s_lw, 16)
            for dst, src in ((x_sb[:, :, 0:TT], xT[:, :, 0:TT]), (wx_sb[:], wx), (b_sb[:], bT)):
                sp.dma_start(dst, src).then_inc(s_xw0, 16)
            for dst, src in ((wr_sb[:], wr), (rb_sb[:], rb), (iota_sb[:], iota), (eye_sb[:], eye),
                             (x_sb[:, :, TT:NTOK], xT[:, :, TT:NTOK])):
                sp.dma_start(dst, src).then_inc(s_in, 16)
            for dst, src in ((sw1_sb, sw1), (sw3_sb, sw3), (sw2_sb, sw2), (rw1_sb, rw1), (rw2_sb, rw2)):
                sp.dma_start(dst[:], src).then_inc(s_mw, 16)
            with sp.Fori(0, NT + 1) as n:
                sp.sem_inc(s_free, 1)
                take_back(sp, s_fin, KC)
                sp.dma_start(outT[:, :, bass.ds(n * TT, TT)], osb[:]).then_inc(s_st, 16)
                take_back(sp, s_st, 16)

        @block.gpsimd
        def _(pool):
            g = nc.gpsimd
            g.memset(x_sb[:, :, NTOK:NTOK + TT], 0.0).then_inc(s_added, 1)
            g.memset(xt[:], 0.0).then_inc(s_xt, 1)
            pool.wait_ge(s_setup, 1)
            g.partition_all_reduce(wtop[:], wmax[:], P, RMAX).then_inc(s_top, 1)
            pool.wait_ge(s_xwc0, MC + 1)
            g.tensor_copy(seeds[:].rearrange("p a s g -> p (a s g)"), xw[:, GATES:(2 * HS + 1) * GATES]).then_inc(s_staged, 2)
            take_back(pool, s_added, 1)
            with pool.Fori(0, NT) as it:
                for q in range(PIECES):
                    pool.wait_ge(s_piece, q + 1)
                    g.tensor_tensor(h_part[:, q % 2].rearrange("p k (s b) -> p k s b", b=B),
                                    h32[:, q % 2, :, :].rearrange("p s (k b) -> p k s b", b=B),
                                    inv_p.rearrange("p (k s b) -> p k s b", k=1, s=1).broadcast_to([P, KC, HS, B]),
                                    ALU.mult).then_inc(s_added, 1)
                    pool.wait_ge(s_added, 2 * q + 1)
                    g.tensor_tensor(x_new[:, :, q * HS * B:(q + 1) * HS * B], h_part[:, q % 2],
                                    x_sb[:, :, bass.ds(it * TT + q * HS * B, HS * B)], ALU.add).then_inc(s_added, 1)
                    g.tensor_copy(seeds[:, q % 2, :, :].rearrange("p s g -> p (s g)"),
                                  xw[:, bass.ds(it * (TS * GATES) + ((q + 2) * HS + 1) * GATES, HS * GATES)]).then_inc(s_staged, 1)
                pool.wait_ge(s_added, 2 * PIECES)
                g.tensor_copy(xt[:], x_new[:]).then_inc(s_xt, 1)
                take_back(pool, s_piece, PIECES)
                take_back(pool, s_added, 2 * PIECES)

        @block.scalar
        def _(act):
            activation = nc.scalar.activation
            nc.scalar.preload_act_table(ACT.Gelu)

            def mixture(s, xw_at=None):
                if s == LT:
                    act.wait_ge(s_lc, 1)
                    activation(rt[:, 1, :], rt[:, 0, :], ACT.Tanh, scale=-1.0 / 64).then_inc(s_lt, 1)
                if s in UP1:
                    act.wait_ge(s_up, UP1[s] + 1)
                    activation(th[:], a1, ACT.Tanh, scale=0.5).then_inc(s_act, 1)
                if s in UP3 and xw_at is not None:
                    m = UP3[s]
                    act.wait_ge(s_xwp, m + 1)
                    activation(xw_at[:, :, m * B:(m + 1) * B], xw_ps.rearrange("p (t b) -> p t b", b=B), ACT.Identity,
                               bias=b_scaled[:, m:m + 1], scale=S0 * (2.0 if m < KC else 1.0)).then_inc(s_xwe, 1)
                if s in UP_R1:
                    act.wait_ge(s_up, NQ + UP_R1[s] + 1)
                    activation(ge[:], up_rt[:, 0:RC * TT].rearrange("p (c t) -> p c t", c=RC), ACT.Gelu).then_inc(s_act, 1)

            with act.Fori(0, NT) as it:
                xw_at = xw[:, bass.ds((it + 1) * (TS * GATES), TS * GATES)].rearrange("p (t g) -> p t g", g=GATES)
                for s in range(TS):
                    act.wait_ge(s_sum, 4 * s + F_OF)
                    activation(tf[:], f_sum, ACT.Tanh, scale=0.5 / S0).then_inc(s_tanh, 1)
                    act.wait_ge(s_sum, 4 * s + GI_OF)
                    activation(gi_out, gi_sum.rearrange("p (g c) -> p g c", g=2), ACT.Tanh, scale=0.5 / S0).then_inc(s_tanh, 1)
                    act.wait_ge(s_sum, 4 * s + O_OF)
                    activation(to[:], o_sum, ACT.Tanh, scale=0.5 / S0).then_inc(s_tanh, 1)
                    act.wait_ge(s_sum, 4 * s + C_OF)
                    activation(tc[:], cs[:, :, 2], ACT.Tanh, scale=0.5).then_inc(s_tanh, 1)
                    mixture(s, xw_at)
                take_back(act, s_sum, 4 * TS)
                take_back(act, s_up, NQ + NE)
                take_back(act, s_xwp, NQ)
                take_back(act, s_lc, 1)
            for s in range(LAST + 1):
                mixture(s)

        @block.vector
        def _(dve):
            v = nc.vector
            done = [0]

            def link(ins):
                done[0] += 1
                ins.then_inc(s_link, 1)
                dve.wait_ge(s_link, done[0])

            dve.wait_ge(s_lw, 32)
            v.tensor_reduce(wmax[:], wh_sb[:], AX.XY, ALU.max, apply_absolute_value=True).then_inc(s_setup, 1)
            dve.wait_ge(s_top, 1)
            link(v.tensor_scalar(sc[:, 3:4], wtop[:], 2.0 ** -40, None, ALU.max))
            link(v.tensor_scalar(sc[:, 4:5].bitcast(U32), sc[:, 3:4].bitcast(U32), 0x7F800000, None, ALU.bitwise_and))
            link(v.reciprocal(sc[:, 5:6], sc[:, 4:5]))
            link(v.tensor_scalar(sc[:, 6:7], sc[:, 5:6], 2.0 ** 13, S0, ALU.mult, ALU.min))
            link(v.tensor_scalar(w_scale, sc[:, 6:7], S0 / 2.0 ** 15, None, ALU.max))
            link(v.tensor_scalar(inv_p, w_scale, 1.0 / S0, None, ALU.mult))
            link(v.reciprocal(sc[:, 7:8], inv_p))
            link(v.tensor_scalar(half_p, sc[:, 7:8], 0.5, None, ALU.mult))
            link(v.tensor_copy(half_p4[:], half_p.broadcast_to([P, OG])))
            for lo, hi, more in ((0, D, 2.0), (D, H4, 1.0)):
                scaled = xw[:, 0:KC * (hi - lo)].rearrange("p (k n) -> p k n", k=KC)
                link(v.tensor_scalar(wh_hi[:, :, lo:hi], wh_sb[:, :, lo:hi], w_scale, more, ALU.mult, ALU.mult))
                link(v.tensor_scalar(scaled, wh_sb[:, :, lo:hi], w_scale, more, ALU.mult, ALU.mult))
                link(v.tensor_tensor(wh_lo[:, :, lo:hi], scaled, wh_hi[:, :, lo:hi], ALU.subtract))
            dve.wait_ge(s_xw0, 48)
            for m in range(MC):
                dve.wait_ge(s_xwp0, m + 1)
                v.tensor_scalar(xw[:, 0:TS * GATES].rearrange("p (t g) -> p t g", g=GATES)[:, :, m * B:(m + 1) * B],
                                (up_sh, up_rt)[m % 2][:, 0:TT].rearrange("p (t b) -> p t b", b=B),
                                b_sb[:, m:m + 1], S0 * (2.0 if m < KC else 1.0), ALU.add, ALU.mult).then_inc(s_xwc0, 1)
            link(v.tensor_scalar(b_scaled[:, 0:KC], b_sb[:, 0:KC], 2.0 * S0, None, ALU.mult))
            link(v.tensor_scalar(b_scaled[:, KC:MC], b_sb[:, KC:MC], S0, None, ALU.mult))
            dve.wait_ge(s_xwp0, MC + 1)
            dve.wait_ge(s_xwc0, MC)
            link(v.tensor_scalar(hw0[:], acc_lg[:, 0:GATES], S0, None, ALU.mult))
            link(v.tensor_scalar(hw0[:, 0:HC], hw0[:, 0:HC], 2.0, None, ALU.mult))
            v.tensor_tensor(xw[:, 0:GATES], xw[:, 0:GATES], hw0[:], ALU.add).then_inc(s_xwc0, 1)
            dve.wait_ge(s_xwc0, MC + 1)
            v.tensor_copy(gif_xw, xw[:, 0:GI + FG].rearrange("p (m b) -> p m b", b=B))
            v.tensor_copy(o_xw, xw[:, GI + FG:GATES].rearrange("p (m b) -> p m b", b=B))
            link(v.memset(fac_add[:], 1.0))
            link(v.memset(fac[:, :, 0], 0.0))
            link(v.memset(c_now[:], 0.0))
            link(v.tensor_copy(cexp[:].rearrange("p k (t b) -> p k t b", b=B),
                               cond_sb[:].rearrange("p (k o b) -> p k o b", k=KC, o=1).broadcast_to([P, KC, TS, B])))
            link(v.memset(x_new[:], 0.0))
            v.memset(hh[:], 0.0).then_inc(s_hhi, 1)
            v.memset(hw0[:], 0.0).then_inc(s_hlo, 1)

            lg, nl, e, num, dn, sg, mask, t0, t1, t2 = (rt[:, j, :] for j in range(10))
            total, guarded, inverse, weight, share, half = (den[:, j:j + 1] for j in range(6))

            def mixture(s, ch):
                def chain(ins):
                    ch[0] += 1
                    ins.then_inc(s_chain, 1)

                def chained():
                    dve.wait_ge(s_chain, ch[0])

                if s == LOGITS:
                    dve.wait_ge(s_lg, 1)
                    v.tensor_scalar(lg, logits, 80.0, -80.0, ALU.min, ALU.max).then_inc(s_lc, 1)
                if s == 4:
                    dve.wait_ge(s_lt, 1)
                    chain(v.tensor_scalar(num, nl, 1.0, None, ALU.add))
                    chain(v.tensor_scalar(dn, nl, -1.0, 1.0, ALU.mult, ALU.add))
                    chained()
                    chain(v.reciprocal(t0, dn))
                if s == 5:
                    chained()
                    chain(v.tensor_tensor(e, num, t0, ALU.mult))
                    chained()
                    chain(v.tensor_tensor(t0, e, e, ALU.mult))
                if s in (7, 8):
                    chained()
                    chain(v.tensor_tensor(e, t0, t0, ALU.mult))
                    chained()
                    chain(v.tensor_tensor(t0, e, e, ALU.mult))
                if s == 10:
                    chained()
                    chain(v.tensor_scalar(t1, t0, 1.0, None, ALU.add))
                    chained()
                    chain(v.reciprocal(sg, t1))
                if s == 11:
                    chained()
                    chain(v.tensor_tensor(t0, sg, rb_sb[:], ALU.add))
                    chained()
                    chain(v.max(m8[:], t0))
                if s == 13:
                    chained()
                    chain(v.max_index(i8[:], m8[:], t0))
                    chained()
                    chain(v.tensor_copy(if8[:], i8[:]))
                if s == 14:
                    chained()
                    chain(v.tensor_scalar(t1, iota_sb[:], if8[:, 0:1], None, ALU.is_equal))
                    chained()
                    chain(v.scalar_tensor_tensor(mask, iota_sb[:], if8[:, 1:2], t1, ALU.is_equal, ALU.add))
                if s == 16:
                    chained()
                    chain(v.tensor_tensor(t0, sg, mask, ALU.mult))
                    chained()
                    chain(v.tensor_reduce(total, t0, AX.X, ALU.add))
                if s == 17:
                    chained()
                    chain(v.tensor_scalar(guarded, total, 1e-9, None, ALU.add))
                    chain(v.tensor_scalar(share, total, 1e-9, 0.25, ALU.is_gt, ALU.mult))
                    chain(v.tensor_scalar(half, total, 1e-9, 0.125, ALU.is_le, ALU.mult))
                if s == 19:
                    chained()
                    chain(v.reciprocal(inverse, guarded))
                    chain(v.tensor_scalar(t1, mask, half, None, ALU.mult))
                if s == 20:
                    chained()
                    chain(v.tensor_tensor(weight, inverse, share, ALU.mult))
                    chained()
                    v.scalar_tensor_tensor(gfull[:], t0, weight, t1, ALU.mult, ALU.add).then_inc(s_gate, 1)
                if s in UP3:
                    q = UP3[s]
                    dve.wait_ge(s_act, q + 1)
                    v.scalar_tensor_tensor(uu[:], th[:], 1.0, a1, ALU.add, ALU.mult).then_inc(s_u, 1)
                    dve.wait_ge(s_up3, q + 1)
                    dve.wait_ge(s_u, q + 1)
                    v.scalar_tensor_tensor(hid_sh[:], uu[:], 1.0 / 16, a3, ALU.mult, ALU.mult).then_inc(s_hs, 1)
                for step, half_of in ((GATE0, 0), (GATE1, 1)):
                    if s in step:
                        ex = step[s]
                        dve.wait_ge(s_act, NQ + ex + 1)
                        v.tensor_tensor(hid_rt[:, ex % 2, half_of, :], ge[:, half_of, :], gb_ps, ALU.mult).then_inc(s_hr, 1)
                if s == LAST:
                    dve.wait_ge(s_dn, 1)
                    dve.wait_ge(s_free, 1)
                if s in (LAST, LAST + 1):
                    k = s - LAST
                    v.tensor_tensor(osb[:, k, :], acc[:, k * TT:(k + 1) * TT], xt[:, k, :], ALU.add).then_inc(s_fin, 1)

            def parts(ps):
                return ps.rearrange("p (m j b) -> p m b j", j=PARTS, b=B)

            with dve.Fori(0, NT):
                ch = [0]
                for s in range(TS):
                    piece, at = s // HS, s % HS
                    dve.wait_ge(s_mul, 3 * s + F_OF)
                    v.tensor_reduce(f_sum.rearrange("p (m b) -> p m b", b=B), parts(f_ps), AX.X, ALU.add).then_inc(s_sum, 1)
                    dve.wait_ge(s_mul, 3 * s + GI_OF)
                    v.tensor_reduce(gi_sum.rearrange("p (m b) -> p m b", b=B), parts(gi_ps), AX.X, ALU.add).then_inc(s_sum, 1)
                    dve.wait_ge(s_tanh, 4 * s + F_OF)
                    v.scalar_tensor_tensor(addend[:, :, 2], tf[:], 1.0, c_now[:], ALU.add, ALU.mult).then_inc(s_own, 1)
                    dve.wait_ge(s_mul, 3 * s + O_OF)
                    v.tensor_reduce(o_sum.rearrange("p (m b) -> p m b", b=B), parts(o_ps), AX.X, ALU.add).then_inc(s_sum, 1)
                    dve.wait_ge(s_tanh, 4 * s + GI_OF)
                    dve.wait_ge(s_own, 3 * s + 1)
                    v.tensor_tensor_scan(cs.rearrange("p c j -> p (c j)"), fac.rearrange("p c j -> p (c j)"),
                                         addend.rearrange("p c j -> p (c j)"), 0.0, ALU.mult, ALU.add).then_inc(s_sum, 1)
                    if at == 0:
                        dve.wait_ge(s_staged, piece + 1)
                    v.tensor_copy(gif_xw, seeds[:, piece % 2, at, 0:GI + FG].rearrange("p (m b) -> p m b", b=B))
                    dve.wait_ge(s_tanh, 4 * s + O_OF)
                    v.scalar_tensor_tensor(to1[:], to[:], 1.0, half_p4[:], ALU.add, ALU.mult).then_inc(s_own, 1)
                    v.tensor_copy(o_xw, seeds[:, piece % 2, at, GI + FG:GATES].rearrange("p (m b) -> p m b", b=B))
                    dve.wait_ge(s_tanh, 4 * s + C_OF)
                    dve.wait_ge(s_own, 3 * s + 2)
                    ht = to1[:].rearrange("p (k b) -> p k b", b=B), tc[:].rearrange("p (k b) -> p k b", b=B)
                    v.tensor_tensor(hh[:, :, 0, :], *ht, ALU.mult).then_inc(s_hhi, 1)
                    h_now = h32[:, piece % 2, at, :]
                    v.tensor_tensor(h_now, to1[:], tc[:], ALU.mult).then_inc(s_own, 1)
                    ins = v.tensor_scalar(c_now[:], cs[:, :, 2], 0.5, None, ALU.mult)
                    if at == HS - 1:
                        ins.then_inc(s_piece, 1)
                    dve.wait_ge(s_own, 3 * s + 3)
                    v.tensor_tensor(hh[:, :, 1, :], h_now.rearrange("p (k b) -> p k b", b=B), hh[:, :, 0, :],
                                    ALU.subtract).then_inc(s_hlo, 1)
                    mixture(s, ch)
                take_back(dve, s_mul, 3 * TS)
                take_back(dve, s_tanh, 4 * TS)
                take_back(dve, s_own, 3 * TS)
                take_back(dve, s_staged, PIECES)
                take_back(dve, s_chain, ch[0])
                for sem_, n in ((s_lg, 1), (s_lt, 1), (s_act, NQ + NE), (s_up3, NQ), (s_u, NQ), (s_dn, 1), (s_free, 1)):
                    take_back(dve, sem_, n)
            ch = [0]
            for s in range(LAST + 2):
                mixture(s, ch)

        @block.tensor
        def _(pe):
            mm = nc.tensor.matmul

            def low(ps, m0, n):
                for j in range(n):
                    for c in range(KC):
                        at = (j * PARTS + 1) * B
                        mm(ps[:, at:at + B], wh_lo[:, c, (m0 + j) * P:(m0 + j + 1) * P], hh[:, c, 0, :],
                           start=(j == 0 and c == 0), stop=False, skip_group_check=True)

            def high(ps, m0, n):
                for j in range(n):
                    for c in range(KC):
                        at = j * PARTS * B
                        last = mm(ps[:, at:at + 2 * B], wh_hi[:, c, (m0 + j) * P:(m0 + j + 1) * P], hh[:, c, :, :],
                                  start=False, stop=True, skip_group_check=True)
                return last

            def product(ps, w, at):
                for c in range(KC):
                    last = mm(ps, w[:, c, at:at + P], xt[:, c, :], start=(c == 0), stop=(c == KC - 1))
                return last

            def down(w, hid, first, last):
                for k in range(KC):
                    ins = mm(acc[:, k * TT:(k + 1) * TT], w[:, k * P:(k + 1) * P], hid, start=(first and k == 0), stop=last,
                             skip_group_check=True)
                return ins

            def mixture(s, x_next=None):
                if s == LOGITS:
                    take_back(pe, s_xt, 1)
                    pe.wait_ge(s_in, 16 * 5)
                    for c in range(KC):
                        mm(logits, xt[:, c, :], wr_sb[:, c, :], start=(c == 0), stop=False)
                    for c in range(KC):
                        last = mm(logits, cexp[:, c, :], wr_sb[:, KC + c, :], start=False, stop=(c == KC - 1))
                    last.then_inc(s_lg, 1)
                    pe.wait_ge(s_mw, 16 * 5)
                if s in UP1:
                    q = UP1[s]
                    if q >= 1:
                        pe.wait_ge(s_hs, q)
                    product(a1, sw1_sb, q * P).then_inc(s_up, 1)
                    if x_next is not None:
                        if q >= 1:
                            pe.wait_ge(s_xwe, q)
                        mm(xw_ps, wx_sb[:, 0, q * P:(q + 1) * P], x_next(0), start=True, stop=False)
                if s in UP3:
                    q = UP3[s]
                    product(a3, sw3_sb, q * P).then_inc(s_up3, 1)
                    if x_next is not None:
                        mm(xw_ps, wx_sb[:, 1, q * P:(q + 1) * P], x_next(1), start=False, stop=True).then_inc(s_xwp, 1)
                if s in DOWN_SH:
                    q = DOWN_SH[s]
                    pe.wait_ge(s_hs, q + 1)
                    down(sw2_sb[:, q, :], hid_sh[:], q == 0, False)
                if s in UP_R0:
                    ex = UP_R0[s]
                    if ex == 0:
                        take_back(pe, s_gate, 1)
                        if x_next is not None:
                            pe.wait_ge(s_xwe, NQ)
                    else:
                        pe.wait_ge(s_hr, RC * ex)
                    mm(gb_ps, gfull[:, ex:ex + 1].broadcast_to([P, P]), eye_sb[:], start=True, stop=True)
                    product(up_rt[:, 0:TT], rw1_sb, ex * HR)
                if s in UP_R1:
                    ex = UP_R1[s]
                    product(up_rt[:, TT:2 * TT], rw1_sb, ex * HR + P).then_inc(s_up, 1)
                for step, half_of in ((DOWN_R0, 0), (DOWN_R1, 1)):
                    if s in step:
                        ex = step[s]
                        pe.wait_ge(s_hr, RC * ex + half_of + 1)
                        last = down(rw2_sb[:, ex * RC + half_of, :], hid_rt[:, ex % 2, half_of, :], False, s == LAST)
                        if s == LAST:
                            last.then_inc(s_dn, 1)

            pe.wait_ge(s_xw0, 48)
            for m in range(MC):
                if m >= 2:
                    pe.wait_ge(s_xwc0, m - 1)
                for c in range(KC):
                    last = mm((up_sh, up_rt)[m % 2][:, 0:TT], wx_sb[:, c, m * P:(m + 1) * P], x_sb[:, c, 0:TT],
                              start=(c == 0), stop=(c == KC - 1))
                last.then_inc(s_xwp0, 1)
            pe.wait_ge(s_lw, 32)
            for m in range(MC):
                for c in range(KC):
                    last = mm(acc_lg[:, m * B:(m + 1) * B], wh_sb[:, c, m * P:(m + 1) * P],
                              cond_sb[:, c * B:(c + 1) * B], start=(c == 0), stop=(c == KC - 1))
            last.then_inc(s_xwp0, 1)

            with pe.Fori(0, NT) as it:
                def x_next(c):
                    return x_sb[:, c, bass.ds((it + 1) * TT, TT)]

                for s in range(TS):
                    pe.wait_ge(s_hhi, s + 1)
                    low(f_ps, 4, 2)
                    low(gi_ps, 0, 4)
                    pe.wait_ge(s_hlo, s + 1)
                    high(f_ps, 4, 2).then_inc(s_mul, 1)
                    high(gi_ps, 0, 4).then_inc(s_mul, 1)
                    low(o_ps, 6, 2)
                    high(o_ps, 6, 2).then_inc(s_mul, 1)
                    mixture(s, x_next)
                take_back(pe, s_hhi, TS)
                take_back(pe, s_hlo, TS)
                take_back(pe, s_xwe, NQ)
                take_back(pe, s_hs, NQ)
                take_back(pe, s_hr, RC * NE)
            for s in range(LAST + 1):
                mixture(s)


def kernel(x, cond_1024, L0_cond_Wx, L0_cond_Wh, L0_cond_b, L1_cond_W_router, L1_cond_router_bias,
           L1_cond_s_w1, L1_cond_s_w3, L1_cond_s_w2, L1_cond_r_w1, L1_cond_r_w2):
    import concourse.bacc as bacc
    from concourse.bass_utils import run_bass_kernel_spmd

    def rows(a):
        a = np.asarray(a)
        return np.ascontiguousarray(a.reshape(a.shape[0] // P, P, -1).transpose(1, 0, 2))

    def gate_order(a):
        a = np.asarray(a)
        return np.concatenate([a[..., 3 * D:], a[..., :3 * D]], axis=-1)

    s_w1, s_w3, s_w2, r_w1, r_w2 = (np.asarray(a) for a in (L1_cond_s_w1, L1_cond_s_w3, L1_cond_s_w2, L1_cond_r_w1, L1_cond_r_w2))
    arrays = {
        "xT": rows(np.asarray(x).transpose(2, 1, 0).reshape(D, NTOK)),
        "condT": rows(np.asarray(cond_1024).T).reshape(P, HC),
        "wx": rows(gate_order(L0_cond_Wx)),
        "wh": rows(gate_order(L0_cond_Wh)),
        "bT": np.ascontiguousarray(gate_order(L0_cond_b).reshape(MC, P).T),
        "wr": rows(np.asarray(L1_cond_W_router).T),
        "rb": np.ascontiguousarray(np.broadcast_to(np.asarray(L1_cond_router_bias), (P, NE))),
        "sw1": rows(s_w1.reshape(FSH, D).T),
        "sw3": rows(s_w3.reshape(FSH, D).T),
        "sw2": rows(s_w2.transpose(0, 2, 1).reshape(FSH, D)),
        "rw1": rows(r_w1.reshape(NE * HR, D).T),
        "rw2": rows(r_w2.transpose(0, 2, 1).reshape(NE * HR, D)),
        "eye": np.eye(P, dtype=np.float32),
        "iota": np.ascontiguousarray(np.broadcast_to(np.arange(NE, dtype=np.float32), (P, NE))),
    }
    nc = bacc.Bacc("TRN2", target_bir_lowering=False, num_devices=1)
    args = [nc.dram_tensor(n, a.shape, mybir.dt.from_np(a.dtype), kind="ExternalInput").ap() for n, a in arrays.items()]
    args.append(nc.dram_tensor("outT", (P, KC, TT + NTOK), F32, kind="ExternalOutput").ap())
    cond_resid_kernel(nc, *args)
    r = run_bass_kernel_spmd(nc, [arrays], core_ids=[0])
    got = r.results[0]["outT"][:, :, TT:]
    return np.ascontiguousarray(got.transpose(1, 0, 2).reshape(D, T, B).transpose(2, 1, 0))
```

```python
from contextlib import ExitStack

import numpy as np

import concourse.bass as bass
from concourse import mybir

ALU = mybir.AluOpType
ACT = mybir.ActivationFunctionType
F32 = mybir.dt.float32
F16 = mybir.dt.float16
U32 = mybir.dt.uint32
AX = mybir.AxisListType
RMAX = bass.bass_isa.ReduceOp.max

P = 128
B, T, D = 2, 1024, 256
KC = D // P
H4 = 4 * D
MC = H4 // P
HC = KC * B
GATES = MC * B
GI, FG, OG = 4 * B, 2 * B, 2 * B
PARTS = 3
LO = 2.0 ** 12
NTOK = B * T
BANK = 512
TS = 64
TT = TS * B
NT = T // TS
HS = 8
PIECES = TS // HS
NE = 8
FSH = 1024
NQ = FSH // P
HR = 256
RC = HR // P
F_OF, GI_OF, O_OF, C_OF = 1, 2, 3, 4
TF_OF, TO_OF, TC_OF = 1, 2, 3
LOGITS = 1
LT = 3
UP1 = {3 * q + 2: q for q in range(NQ)}
UP3 = {3 * q + 3: q for q in range(NQ)}
SILU = {3 * q + 3: q for q in range(NQ)}
TIMES = {3 * q + 4: q for q in range(NQ)}
DOWN_SH = {3 * q + 7 if q < NQ - 1 else 3 * q + 8: q for q in range(NQ)}
SPREAD = {26: 0, 34: 1, 43: 2, 48: 3}
ROUTED = (27, 30, 35, 39, 44, 49, 53, 57)
UP_R0 = {s: e for e, s in enumerate(ROUTED)}
UP_R1 = {s + 1: e for e, s in enumerate(ROUTED)}
GATE = {s + 2: e for e, s in enumerate(ROUTED)}
DOWN_R0 = {s + 2: e for e, s in enumerate(ROUTED[1:] + (ROUTED[-1] + 2,))}
DOWN_R1 = {s + 1: e for s, e in DOWN_R0.items()}
LAST = max(DOWN_R1)
MF = MC // 2
XW_FIRST = [(1, m) for m in range(MC)] + [(n, m) for n in range(2, NT) for m in range(MF)]
TERMS = ((0, 0), (0, 1), (1, 0))
PIECES_XW = [(m, c, j) for m in range(MF, MC) for c in range(KC) for j in range(len(TERMS))]
PER = KC * len(TERMS)
XW = {0: PIECES_XW[:PER], 4: PIECES_XW[PER:2 * PER]}
XW.update({5 + i: [p] for i, p in enumerate(PIECES_XW[2 * PER:])})
XW_END = {s: p[-1][0] for s, p in XW.items() if p[-1][1:] == (KC - 1, len(TERMS) - 1)}
XMAX_N = 256
NX, NW = KC * NTOK // XMAX_N, KC * H4 // XMAX_N
MAX_OF = NX + NW
SCALES = MAX_OF + 10
HI = {SCALES + 2 + i: i for i in range(NW)}
LO_OF = {SCALES + 3 + i: i for i in range(2 * NW)}
SPLIT_AT = 5
STAGE_AT = 6


def cond_resid_kernel(nc, xT, condT, wx, wh, bT, wr, rb, sw1, sw3, sw2, rw1, rw2, eye, iota, outT):
    with ExitStack() as ctx:
        def sb(name, shape, dt=F32):
            return ctx.enter_context(nc.sbuf_tensor(name, shape, dt))

        def sem(name):
            return ctx.enter_context(nc.semaphore(name))

        def bank(name, n=1):
            return ctx.enter_context(nc.psum_tensor(name, [P, n * BANK], F32))

        gates = bank("gates", 3)
        state, up_sh, up_rt, acc_lg, xw_next = (bank(n) for n in ("state", "up_sh", "up_rt", "acc_lg", "xw_next"))
        gi_ps = gates[:, BANK - PARTS * GI:BANK]
        f_ps = gates[:, BANK:BANK + PARTS * FG]
        o_ps = gates[:, 2 * BANK:2 * BANK + PARTS * OG]
        gif_xw = gates[:, BANK - PARTS * GI:BANK + PARTS * FG].rearrange("p (c j) -> p c j", j=PARTS)[:, :, 2]
        o_xw = o_ps.rearrange("p (c j) -> p c j", j=PARTS)[:, :, 2]
        gi_sum = gates[:, 0:PARTS * GI]
        f_sum = gates[:, 2 * BANK - PARTS * FG:2 * BANK]
        o_sum = gates[:, 3 * BANK - PARTS * OG:3 * BANK]
        cs = state[:, 0:HC * 3].rearrange("p (c j) -> p c j", j=3)
        xw_first = [xw_next[:, 0:TT], up_rt[:, 0:TT]]
        a1, a3 = up_sh[:, 0:TT], up_rt[:, 0:TT]
        acc = acc_lg[:, 0:KC * TT]
        logits = acc_lg[:, KC * TT:KC * TT + NE]
        gb_ps = [up_sh[:, j * TT:(j + 1) * TT] for j in range(4)]

        x_sb = sb("x_sb", [P, KC, NTOK + 2 * TT])
        xw = sb("xw", [P, (T + TS) * GATES])
        cond_sb = sb("cond_sb", [P, HC])
        wx_sb = sb("wx_sb", [P, KC, H4])
        wh_sb = sb("wh_sb", [P, KC, H4])
        wh_hi = sb("wh_hi", [P, KC, H4], F16)
        wh_lo = sb("wh_lo", [P, KC, H4], F16)
        wx_part = [sb("wx_hi", [P, KC, H4], F16), sb("wx_lo", [P, KC, H4], F16)]
        x_scaled = sb("x_scaled", [P, KC, TT])
        x_part = [sb("x_hi", [P, KC, TT], F16), sb("x_lo", [P, KC, TT], F16)]
        b_sb = sb("b_sb", [P, MC])
        b_twice = sb("b_twice", [P, KC])
        wr_sb = sb("wr_sb", [P, 2 * KC, NE])
        rb_sb = sb("rb_sb", [P, NE])
        sw1_sb = sb("sw1_sb", [P, KC, FSH])
        sw3_sb = sb("sw3_sb", [P, KC, FSH])
        sw2_sb = sb("sw2_sb", [P, NQ, D])
        rw1_sb = sb("rw1_sb", [P, KC, NE * HR])
        rw2_sb = sb("rw2_sb", [P, NE * RC, D])
        eye_sb = sb("eye_sb", [P, P])
        iota_sb = sb("iota_sb", [P, NE])

        wmax = sb("wmax", [P, 3])
        wtop = sb("wtop", [P, 3])
        scale = sb("scale", [P, 4, 3])
        s_wh, s_wx, s_xin = scale[:, 3, 0:1], scale[:, 3, 1:2], scale[:, 3, 2:3]
        sc = sb("sc", [P, 6])
        unit, one_unit, half_lo, s_wh_lo, wh_g, wh_g_lo = (sc[:, j:j + 1] for j in range(6))
        xw_scale = sb("xw_scale", [P, 2])
        largest = sb("largest", [P, MAX_OF])
        first_banks = (up_sh, up_rt, xw_next, state)
        wh_times_lo = xw[:, TS * GATES:TS * GATES + KC * H4].rearrange("p (k n) -> p k n", k=KC)
        hw0 = sb("hw0", [P, GATES])
        hh = sb("hh", [P, KC, B, 2], F16)
        h32 = sb("h32", [P, 2, HS, HC])
        seeds = sb("seeds", [P, 2, HS, GATES])
        part_fac = sb("part_fac", [P, GI, PARTS])
        fac_add = sb("fac_add", [P, 2, HC, 3])
        fac, addend = fac_add[:, 0, :, :], fac_add[:, 1, :, :]
        gi_out = fac_add[:].rearrange("p a c j -> p (a c j)")[:, 2:2 + 2 * (HC * 3 - 1)].rearrange(
            "p (a z) -> p a z", a=2)[:, :, 0:HC * 3 - 2:3]
        tf = sb("tf", [P, FG])
        tc = sb("tc", [P, HC])
        c_now = sb("c_now", [P, HC])
        to = sb("to", [P, OG])
        to1 = sb("to1", [P, OG])

        tpart = sb("tpart", [P, NE])
        cexp = sb("cexp", [P, KC, TT])
        h_part = sb("h_part", [P, 2, KC, HS * B])
        x_new = sb("x_new", [P, KC, TT])
        xt = sb("xt", [P, KC, TT])
        rt = sb("rt", [P, 9, NE])
        m8 = sb("m8", [P, 8])
        i8 = sb("i8", [P, 8], U32)
        if8 = sb("if8", [P, 8])
        den = sb("den", [P, 6])
        gfull = sb("gfull", [P, NE])
        th = sb("th", [P, TT])
        uu = sb("uu", [P, 2, TT])
        hid_sh = sb("hid_sh", [P, 2, TT])
        ge = sb("ge", [P, RC, TT])
        hid_rt = sb("hid_rt", [P, 2, RC, TT])
        osb = sb("osb", [P, KC, TT])

        s_lw, s_xw0, s_x = sem("wh_loaded"), sem("wx_loaded"), sem("x_loaded")
        s_in, s_mw = sem("router_loaded"), sem("moe_weights_loaded")
        s_scale, s_hi, s_lo = sem("scales_ready"), sem("weights_hi_ready"), sem("weights_lo_ready")
        s_xmax, s_wxs = sem("x_looked_over"), sem("wx_scale_ready")
        s_parts, s_xpart = sem("next_x_scaled"), sem("next_x_in_parts")
        s_link, s_own = sem("vector_setup_step"), sem("vector_step_done")
        s_setup = sem("vector_setup_done")
        s_top = sem("max_over_partitions")
        s_xwp0, s_xwc0 = sem("first_xw_product"), sem("first_xw_copied")
        s_hhi, s_hlo = sem("h_hi_ready"), sem("h_lo_ready")
        s_mul, s_sum, s_tanh = sem("f_gi_o_multiplied"), sem("f_gi_o_c_summed"), sem("f_o_c_tanh")
        s_scan = sem("scan_operands_ready")
        s_piece, s_staged, s_added = sem("piece_of_steps_done"), sem("piece_staged"), sem("h_added_to_x")
        s_xt = sem("tile_copied")
        s_xwp, s_xwe = sem("xw_product"), sem("xw_copied")
        s_cond = sem("cond_spread")
        s_lg, s_lc, s_lt = sem("logits"), sem("logits_clamped"), sem("logits_tanh")
        s_chain = sem("vector_router_step")
        s_gate = sem("gates_ready")
        s_up, s_up3, s_act = sem("up_for_scalar"), sem("up_w3_done"), sem("activated")
        s_hs, s_hr = sem("shared_hidden_step"), sem("routed_hidden_ready")
        s_dn = sem("mixture_summed")
        s_fin, s_st, s_free = sem("tile_finished"), sem("tile_stored"), sem("output_buffer_free")

        def wx_slice(w, i, n):
            w = w[:].rearrange("p k g -> p (k g)")
            return w[:, i * KC * H4 // n:(i + 1) * KC * H4 // n]

        def take_back(eng, s, n):
            eng.wait_ge(s, n)
            eng.sem_inc(s, -n)

        block = ctx.enter_context(nc.Block())

        @block.sync
        def _(sp):
            for dst, src in ((wh_sb[:], wh), (cond_sb[:], condT)):
                sp.dma_start(dst, src).then_inc(s_lw, 16)
            for dst, src in ((x_sb[:, :, 0:TT], xT[:, :, 0:TT]), (wx_sb[:], wx), (b_sb[:], bT)):
                sp.dma_start(dst, src).then_inc(s_xw0, 16)
            for dst, src in ((wr_sb[:], wr), (rb_sb[:], rb), (iota_sb[:], iota), (eye_sb[:], eye)):
                sp.dma_start(dst, src).then_inc(s_in, 16)
            sp.dma_start(x_sb[:, :, TT:NTOK], xT[:, :, TT:NTOK]).then_inc(s_x, 16)
            for dst, src in ((sw1_sb, sw1), (sw3_sb, sw3), (sw2_sb, sw2), (rw1_sb, rw1), (rw2_sb, rw2)):
                sp.dma_start(dst[:], src).then_inc(s_mw, 16)
            with sp.Fori(0, NT) as n:
                sp.sem_inc(s_free, 1)
                take_back(sp, s_fin, 1)
                sp.dma_start(outT[:, :, bass.ds(n * TT, TT)], osb[:]).then_inc(s_st, 16)
                take_back(sp, s_st, 16)

        @block.gpsimd
        def _(pool):
            g = nc.gpsimd
            g.memset(x_sb[:, :, NTOK:NTOK + 2 * TT], 0.0).then_inc(s_added, 1)
            g.memset(xw[:, T * GATES:(T + TS) * GATES], 0.0).then_inc(s_added, 1)
            pool.wait_ge(s_setup, 1)
            g.partition_all_reduce(wtop[:, 0:1], wmax[:, 0:1], P, RMAX).then_inc(s_top, 1)
            pool.wait_ge(s_xwc0, MC + 1)
            take_back(pool, s_added, 2)

            def stage(q, first):
                g.tensor_copy(seeds[:, q % 2, :, :].rearrange("p s g -> p (s g)"), xw[:, first]).then_inc(s_staged, 1)

            stage(0, slice(GATES, (HS + 1) * GATES))

            def split(at):
                g.tensor_tensor(x_scaled[:], x_sb[:, :, at], s_xin.rearrange("p (k t) -> p k t", k=1).broadcast_to([P, KC, TT]),
                                ALU.mult).then_inc(s_parts, 1)
                pool.wait_ge(s_parts, 1)
                g.tensor_copy(x_part[0][:], x_scaled[:]).then_inc(s_parts, 1)
                take_back(pool, s_parts, 2)
                g.tensor_tensor(x_part[1][:], x_scaled[:], x_part[0][:], ALU.subtract).then_inc(s_xpart, 1)

            def piece(q, tile):
                pool.wait_ge(s_piece, 2 * q + 1)
                first = tile * (TS * GATES) + ((q + 1) * HS + 1) * GATES
                stage(q + 1, bass.ds(first, HS * GATES))
                pool.wait_ge(s_piece, 2 * q + 2)
                g.tensor_tensor(h_part[:, q % 2].rearrange("p k (s b) -> p k s b", b=B),
                                h32[:, q % 2, :, :].rearrange("p s (k b) -> p k s b", b=B),
                                half_lo.rearrange("p (k s b) -> p k s b", k=1, s=1).broadcast_to([P, KC, HS, B]),
                                ALU.mult).then_inc(s_added, 1)
                pool.wait_ge(s_added, 2 * q + 1)
                g.tensor_tensor(x_new[:, :, q * HS * B:(q + 1) * HS * B], h_part[:, q % 2],
                                x_sb[:, :, bass.ds(tile * TT + q * HS * B, HS * B)], ALU.add).then_inc(s_added, 1)

            def finish():
                pool.wait_ge(s_added, 2 * PIECES)
                g.tensor_copy(xt[:], x_new[:]).then_inc(s_xt, 1)
                take_back(pool, s_piece, 2 * PIECES)
                take_back(pool, s_added, 2 * PIECES)

            for q in range(PIECES):
                piece(q, 0)
                if q == MAX_OF // HS:
                    pool.wait_ge(s_setup, 3)
                    g.partition_all_reduce(wtop[:, 1:3], wmax[:, 1:3], P, RMAX).then_inc(s_top, 1)
                if q == SPLIT_AT:
                    split(slice(2 * TT, 3 * TT))
            finish()
            with pool.Fori(1, NT) as it:
                for q in range(PIECES):
                    piece(q, it)
                    if q == SPLIT_AT:
                        split(bass.ds((it + 2) * TT, TT))
                finish()

        @block.scalar
        def _(act):
            activation = nc.scalar.activation
            nc.scalar.preload_act_table(ACT.Gelu)
            act.wait_ge(s_scale, 4)
            for dst, dst_lo, src, by, by_lo in ((wh_hi[:, :, 0:D], wh_times_lo[:, :, 0:D], wh_sb[:, :, 0:D], wh_g, wh_g_lo),
                                                (wh_hi[:, :, D:H4], wh_times_lo[:, :, D:H4], wh_sb[:, :, D:H4], s_wh, s_wh_lo)):
                activation(dst, src, ACT.Identity, scale=by)
                activation(dst_lo, src, ACT.Identity, scale=by_lo).then_inc(s_hi, 1)

            def lstm(s):
                act.wait_ge(s_sum, 4 * s + F_OF)
                activation(tf[:], f_sum.rearrange("p (c j) -> p c j", j=PARTS)[:, :, PARTS - 1], ACT.Tanh, scale=0.5).then_inc(s_tanh, 1)
                act.wait_ge(s_sum, 4 * s + GI_OF)
                activation(gi_out, gi_sum.rearrange("p (g c j) -> p g c j", g=2, j=PARTS)[:, :, :, PARTS - 1], ACT.Tanh,
                           scale=0.5).then_inc(s_scan, 1)
                act.wait_ge(s_sum, 4 * s + O_OF)
                activation(to[:], o_sum.rearrange("p (c j) -> p c j", j=PARTS)[:, :, PARTS - 1], ACT.Tanh, scale=0.5).then_inc(s_tanh, 1)
                act.wait_ge(s_sum, 4 * s + C_OF)
                activation(tc[:], cs[:, :, 2], ACT.Tanh, scale=0.5).then_inc(s_tanh, 1)

            def first_tile(s):
                if s < len(XW_FIRST):
                    n, m = XW_FIRST[s]
                    act.wait_ge(s_xwp, s + 1)
                    activation(xw[:, n * TS * GATES:(n + 1) * TS * GATES].rearrange("p (t g) -> p t g", g=GATES)[:, :, m * B:(m + 1) * B],
                               xw_first[s % 2].rearrange("p (t b) -> p t b", b=B), ACT.Identity,
                               bias=b_twice[:, m:m + 1] if m < KC else b_sb[:, m:m + 1], scale=2.0 if m < KC else 1.0).then_inc(s_xwe, 1)
                if s in HI:
                    if HI[s] == 0:
                        act.wait_ge(s_wxs, 1)
                    activation(wx_slice(wx_part[0], HI[s], NW), wx_slice(wx_sb, HI[s], NW), ACT.Identity, scale=s_wx).then_inc(s_hi, 1)

            def mixture(s, xw_at=None):
                if s == LT:
                    act.wait_ge(s_lc, 1)
                    activation(rt[:, 1, :], rt[:, 0, :], ACT.Tanh, scale=-1.0 / 64).then_inc(s_lt, 1)
                if s in UP1:
                    act.wait_ge(s_up, UP1[s] + 1)
                    activation(th[:], a1, ACT.Tanh, scale=0.5).then_inc(s_act, 1)
                if s in XW_END and xw_at is not None:
                    m = XW_END[s]
                    act.wait_ge(s_xwp, m - MF + 1)
                    activation(xw_at[:, :, m * B:(m + 1) * B], xw_next[:, 0:TT].rearrange("p (t b) -> p t b", b=B), ACT.Identity,
                               bias=b_sb[:, m:m + 1], scale=xw_scale[:, 0:1]).then_inc(s_xwe, 1)
                if s in UP_R1:
                    act.wait_ge(s_up, NQ + UP_R1[s] + 1)
                    activation(ge[:], up_rt[:, 0:RC * TT].rearrange("p (c t) -> p c t", c=RC), ACT.Gelu).then_inc(s_act, 1)

            for s in range(TS):
                lstm(s)
                first_tile(s)
            take_back(act, s_sum, 4 * TS)
            take_back(act, s_xwp, len(XW_FIRST))
            with act.Fori(1, NT) as it:
                xw_at = xw[:, bass.ds((it + 1) * (TS * GATES), TS * GATES)].rearrange("p (t g) -> p t g", g=GATES)
                for s in range(TS):
                    lstm(s)
                    mixture(s, xw_at)
                take_back(act, s_sum, 4 * TS)
                take_back(act, s_up, NQ + NE)
                take_back(act, s_xwp, MC - MF)
                take_back(act, s_lc, 1)
            for s in range(LAST + 1):
                mixture(s)

        @block.vector
        def _(dve):
            v = nc.vector
            done = [0]

            def link(ins):
                done[0] += 1
                ins.then_inc(s_link, 1)
                dve.wait_ge(s_link, done[0])

            def power(at, *more):
                link(v.tensor_scalar(scale[:, 0, at], wtop[:, at], 2.0 ** -40, None, ALU.max))
                for ins in more:
                    link(ins())
                link(v.tensor_scalar(scale[:, 1, at].bitcast(U32), scale[:, 0, at].bitcast(U32), 0x7F800000, None, ALU.bitwise_and))
                link(v.reciprocal(scale[:, 2, at], scale[:, 1, at]))
                link(v.tensor_scalar(scale[:, 3, at], scale[:, 2, at], 2.0 ** 13, None, ALU.mult))

            link(v.memset(part_fac[:], 1.0))
            link(v.memset(part_fac[:, :, 0], 0.0))
            link(v.memset(part_fac[:, :, 1], 1.0 / LO))
            link(v.memset(fac_add[:], 1.0))
            link(v.memset(fac[:, :, 0], 0.0))
            link(v.memset(c_now[:], 0.0))
            link(v.memset(half_lo, 0.5 / LO))
            link(v.memset(hh[:], 0.0))
            dve.wait_ge(s_lw, 32)
            v.tensor_reduce(wmax[:, 0:1], wh_sb[:], AX.XY, ALU.max, apply_absolute_value=True).then_inc(s_setup, 1)
            dve.wait_ge(s_xwp0, 1)
            link(v.tensor_copy(hw0[:], acc_lg[:, 0:GATES]))
            link(v.tensor_scalar(hw0[:, 0:HC], hw0[:, 0:HC], 2.0, None, ALU.mult))
            v.tensor_copy(cexp[:].rearrange("p k (t b) -> p k t b", b=B),
                          cond_sb[:].rearrange("p (k o b) -> p k o b", k=KC, o=1).broadcast_to([P, KC, TS, B])).then_inc(s_cond, 1)
            dve.wait_ge(s_top, 1)
            power(slice(0, 1))
            for dst, src, by in ((unit, s_wh, 2.0), (s_wh_lo, s_wh, LO), (wh_g, s_wh, 2.0)):
                v.tensor_scalar(dst, src, by, None, ALU.mult).then_inc(s_scale, 1)
            v.tensor_scalar(wh_g_lo, s_wh, 2.0 * LO, None, ALU.mult).then_inc(s_scale, 1)
            dve.wait_ge(s_scale, 4)
            link(v.reciprocal(one_unit, unit))
            link(v.tensor_copy(part_fac[:, :, 2], one_unit.broadcast_to([P, GI])))
            dve.wait_ge(s_xw0, 48)
            link(v.tensor_scalar(b_twice[:], b_sb[:, 0:KC], 2.0, None, ALU.mult))

            def first_xw(m):
                dve.wait_ge(s_xwp0, m + 2)
                v.tensor_scalar(xw[:, 0:TS * GATES].rearrange("p (t g) -> p t g", g=GATES)[:, :, m * B:(m + 1) * B],
                                first_banks[m % len(first_banks)][:, 0:TT].rearrange("p (t b) -> p t b", b=B),
                                b_sb[:, m:m + 1], 2.0 if m < KC else 1.0, ALU.add, ALU.mult).then_inc(s_xwc0, 1)

            for j, (lo, hi, chunks) in enumerate(((0, D, range(0, 4)), (D, H4, range(4, MC)))):
                for m in chunks:
                    first_xw(m)
                dve.wait_ge(s_hi, j + 1)
                v.scalar_tensor_tensor(wh_lo[:, :, lo:hi], wh_hi[:, :, lo:hi], -LO, wh_times_lo[:, :, lo:hi],
                                       ALU.mult, ALU.add).then_inc(s_lo, 1)
            dve.wait_ge(s_xwc0, MC)
            v.tensor_tensor(xw[:, 0:GATES], xw[:, 0:GATES], hw0[:], ALU.add).then_inc(s_xwc0, 1)
            take_back(dve, s_lg, 1)
            link(v.tensor_copy(tpart[:], logits))
            dve.wait_ge(s_xwc0, MC + 1)
            v.tensor_copy(gif_xw, xw[:, 0:GI + FG])
            v.tensor_copy(o_xw, xw[:, GI + FG:GATES]).then_inc(s_hhi, 1)
            v.memset(hw0[:], 0.0).then_inc(s_hlo, 1)

            lg, nl, e, num, dn, sg, mask, t0, t1 = (rt[:, j, :] for j in range(9))
            total, guarded, inverse, weight, share, half = (den[:, j:j + 1] for j in range(6))

            def mixture(s, ch):
                def chain(ins):
                    ch[0] += 1
                    ins.then_inc(s_chain, 1)

                def chained():
                    dve.wait_ge(s_chain, ch[0])

                if s == LOGITS:
                    take_back(dve, s_lg, 1)
                    chain(v.tensor_tensor(t0, logits, tpart[:], ALU.add))
                    chained()
                    v.tensor_scalar(lg, t0, 80.0, -80.0, ALU.min, ALU.max).then_inc(s_lc, 1)
                if s == 4:
                    take_back(dve, s_lt, 1)
                    chain(v.tensor_scalar(num, nl, 1.0, None, ALU.add))
                    chain(v.tensor_scalar(dn, nl, -1.0, 1.0, ALU.mult, ALU.add))
                elif s in (5, 7, 8, 10, 11, 13, 14, 16, 17, 19, 20):
                    chained()
                if s == 5:
                    chain(v.tensor_tensor(e, num, t0, ALU.mult))
                if s in (7, 8):
                    chain(v.tensor_tensor(e, t0, t0, ALU.mult))
                if s == 10:
                    chain(v.tensor_scalar(t1, t0, 1.0, None, ALU.add))
                if s == 11:
                    chain(v.tensor_tensor(t0, sg, rb_sb[:], ALU.add))
                if s == 13:
                    chain(v.max_index(i8[:], m8[:], t0))
                if s == 14:
                    chain(v.tensor_scalar(t1, iota_sb[:], if8[:, 0:1], None, ALU.is_equal))
                if s == 16:
                    chain(v.tensor_tensor(t0, sg, mask, ALU.mult))
                if s == 17:
                    chain(v.tensor_scalar(guarded, total, 1e-9, None, ALU.add))
                    chain(v.tensor_scalar(share, total, 1e-9, 0.25, ALU.is_gt, ALU.mult))
                    chain(v.tensor_scalar(half, total, 1e-9, 0.125, ALU.is_le, ALU.mult))
                if s == 19:
                    chain(v.reciprocal(inverse, guarded))
                    chain(v.tensor_scalar(t1, mask, half, None, ALU.mult))
                if s == 20:
                    chain(v.tensor_tensor(weight, inverse, share, ALU.mult))

                if s in SILU:
                    q = SILU[s]
                    dve.wait_ge(s_act, q + 1)
                    v.scalar_tensor_tensor(uu[:, q % 2, :], th[:], 1.0, a1, ALU.add, ALU.mult).then_inc(s_hs, 1)
                if s in TIMES:
                    q = TIMES[s]
                    dve.wait_ge(s_up3, q + 1)
                    dve.wait_ge(s_hs, 2 * q + 1)
                    v.scalar_tensor_tensor(hid_sh[:, q % 2, :], uu[:, q % 2, :], 1.0 / 16, a3, ALU.mult, ALU.mult).then_inc(s_hs, 1)
                if s in GATE:
                    ex = GATE[s]
                    dve.wait_ge(s_act, NQ + ex + 1)
                    v.tensor_tensor(hid_rt[:, ex % 2, :, :], ge[:], gb_ps[ex % 4].rearrange("p (c t) -> p c t", c=1).broadcast_to(
                        [P, RC, TT]), ALU.mult).then_inc(s_hr, 1)

                if s in (4, 5, 7, 8, 10, 11, 13, 14, 16, 20):
                    chained()
                if s == 4:
                    chain(v.reciprocal(t0, dn))
                if s in (5, 7, 8):
                    chain(v.tensor_tensor(t0, e, e, ALU.mult))
                if s == 10:
                    chain(v.reciprocal(sg, t1))
                if s == 11:
                    chain(v.max(m8[:], t0))
                if s == 13:
                    chain(v.tensor_copy(if8[:], i8[:]))
                if s == 14:
                    chain(v.scalar_tensor_tensor(mask, iota_sb[:], if8[:, 1:2], t1, ALU.is_equal, ALU.add))
                if s == 16:
                    chain(v.tensor_reduce(total, t0, AX.X, ALU.add))
                if s == 20:
                    v.scalar_tensor_tensor(gfull[:], t0, weight, t1, ALU.mult, ALU.add).then_inc(s_gate, 1)
                    take_back(dve, s_chain, ch[0])
                if s == LAST - 1:
                    take_back(dve, s_act, NQ + NE)
                    take_back(dve, s_up3, NQ)
                if s == LAST:
                    take_back(dve, s_dn, 1)
                    take_back(dve, s_free, 1)
                    v.tensor_tensor(osb[:], acc.rearrange("p (k t) -> p k t", k=KC), xt[:], ALU.add).then_inc(s_fin, 1)

            def summed(dst, ps, n):
                return v.tensor_tensor_scan(dst, part_fac[:, 0:n, :].rearrange("p c j -> p (c j)"), ps, 0.0, ALU.mult, ALU.add)

            def lstm(s):
                piece, at = s // HS, s % HS
                dve.wait_ge(s_mul, 3 * s + F_OF)
                summed(f_sum, f_ps, FG).then_inc(s_sum, 1)
                dve.wait_ge(s_mul, 3 * s + GI_OF)
                summed(gi_sum, gi_ps, GI).then_inc(s_sum, 1)
                dve.wait_ge(s_tanh, 3 * s + TF_OF)
                v.scalar_tensor_tensor(addend[:, :, 2], tf[:], 1.0, c_now[:], ALU.add, ALU.mult).then_inc(s_scan, 1)
                dve.wait_ge(s_mul, 3 * s + O_OF)
                summed(o_sum, o_ps, OG).then_inc(s_sum, 1)
                dve.wait_ge(s_scan, 2 * s + 2)
                v.tensor_tensor_scan(cs.rearrange("p c j -> p (c j)"), fac.rearrange("p c j -> p (c j)"),
                                     addend.rearrange("p c j -> p (c j)"), 0.0, ALU.mult, ALU.add).then_inc(s_sum, 1)
                if at == 0:
                    dve.wait_ge(s_staged, piece + 1)
                v.tensor_copy(gif_xw, seeds[:, piece % 2, at, 0:GI + FG])
                dve.wait_ge(s_tanh, 3 * s + TO_OF)
                v.tensor_scalar(to1[:], to[:], 1.0, LO, ALU.add, ALU.mult).then_inc(s_own, 1)
                dve.wait_ge(s_tanh, 3 * s + TC_OF)
                v.scalar_tensor_tensor(hh[:, :, :, 1], to[:].rearrange("p (k b) -> p k b", b=B), 1.0,
                                       tc[:].rearrange("p (k b) -> p k b", b=B), ALU.add, ALU.mult).then_inc(s_hhi, 1)
                h_now = h32[:, piece % 2, at, :]
                dve.wait_ge(s_own, 2 * s + 1)
                v.tensor_tensor(h_now, to1[:], tc[:], ALU.mult).then_inc(s_own, 1)
                ins = v.tensor_scalar(c_now[:], cs[:, :, 2], 0.5, None, ALU.mult)
                if at in (STAGE_AT, HS - 1):
                    ins.then_inc(s_piece, 1)
                v.tensor_copy(o_xw, seeds[:, piece % 2, at, GI + FG:GATES])
                dve.wait_ge(s_own, 2 * s + 2)
                v.scalar_tensor_tensor(hh[:, :, :, 0], hh[:, :, :, 1], -LO, h_now.rearrange("p (k b) -> p k b", b=B),
                                       ALU.mult, ALU.add).then_inc(s_hlo, 1)

            def round_end():
                take_back(dve, s_mul, 3 * TS)
                take_back(dve, s_tanh, 3 * TS)
                take_back(dve, s_scan, 2 * TS)
                take_back(dve, s_own, 2 * TS)
                take_back(dve, s_staged, PIECES)
            def first_tile(s):
                if s == 0:
                    dve.wait_ge(s_x, 16)
                if s < MAX_OF:
                    k, t = divmod(s * XMAX_N, NTOK)
                    src = x_sb[:, k, t:t + XMAX_N] if s < NX else wx_slice(wx_sb, s - NX, NW)
                    v.tensor_reduce(largest[:, s:s + 1], src, AX.X, ALU.max, apply_absolute_value=True).then_inc(s_xmax, 1)
                if s == MAX_OF:
                    dve.wait_ge(s_xmax, MAX_OF)
                    v.tensor_reduce(wmax[:, 1:2], largest[:, NX:MAX_OF], AX.X, ALU.max).then_inc(s_setup, 1)
                    v.tensor_reduce(wmax[:, 2:3], largest[:, 0:NX], AX.X, ALU.max).then_inc(s_setup, 1)
                if s == SCALES:
                    dve.wait_ge(s_top, 2)
                    power(slice(1, 3), lambda: v.tensor_scalar(scale[:, 0, 2:3], scale[:, 0, 2:3], 1.0, None, ALU.add))
                if s == SCALES + 1:
                    link(v.tensor_tensor(xw_scale[:, 1:2], s_wx, s_xin, ALU.mult))
                    v.reciprocal(xw_scale[:, 0:1], xw_scale[:, 1:2]).then_inc(s_wxs, 1)
                if s in LO_OF:
                    i = LO_OF[s]
                    dve.wait_ge(s_hi, 2 + i // 2 + 1)
                    v.scalar_tensor_tensor(wx_slice(wx_part[1], i, 2 * NW), wx_slice(wx_sb, i, 2 * NW), s_wx,
                                           wx_slice(wx_part[0], i, 2 * NW), ALU.mult, ALU.subtract).then_inc(s_lo, 1)

            for s in range(TS):
                lstm(s)
                first_tile(s)
            round_end()
            with dve.Fori(1, NT):
                ch = [0]
                for s in range(TS):
                    lstm(s)
                    mixture(s, ch)
                round_end()
            ch = [0]
            for s in range(LAST + 1):
                mixture(s, ch)

        @block.tensor
        def _(pe):
            mm = nc.tensor.matmul

            def columns(ps, j):
                return ps[:, j * PARTS * B:(j + 1) * PARTS * B].rearrange("p (b j) -> p b j", j=PARTS)

            def low(ps, m0, n):
                for j in range(n):
                    for c in range(KC):
                        mm(columns(ps, j)[:, :, 0], wh_lo[:, c, (m0 + j) * P:(m0 + j + 1) * P], hh[:, c, :, 1],
                           start=(j == 0 and c == 0), stop=False, skip_group_check=True)

            def high(ps, m0, n):
                for j in range(n):
                    for c in range(KC):
                        last = mm(columns(ps, j)[:, :, 0:2], wh_hi[:, c, (m0 + j) * P:(m0 + j + 1) * P], hh[:, c, :, :],
                                  start=False, stop=True, skip_group_check=True)
                return last

            def product(ps, w, at):
                for c in range(KC):
                    last = mm(ps, w[:, c, at:at + P], xt[:, c, :], start=(c == 0), stop=(c == KC - 1))
                return last

            def down(w, hid, first, last):
                for k in range(KC):
                    ins = mm(acc[:, k * TT:(k + 1) * TT], w[:, k * P:(k + 1) * P], hid, start=(first and k == 0), stop=last,
                             skip_group_check=True)
                return ins

            def mixture(s, with_xw):
                if s == LOGITS:
                    take_back(pe, s_xt, 1)
                    for c in range(KC):
                        last = mm(logits, xt[:, c, :], wr_sb[:, c, :], start=(c == 0), stop=(c == KC - 1))
                    last.then_inc(s_lg, 1)
                if s in UP1:
                    q = UP1[s]
                    if q >= 1:
                        pe.wait_ge(s_hs, 2 * q - 1)
                    product(a1, sw1_sb, q * P).then_inc(s_up, 1)
                if s in UP3:
                    q = UP3[s]
                    if q >= 1:
                        pe.wait_ge(s_hs, 2 * q)
                    product(a3, sw3_sb, q * P).then_inc(s_up3, 1)
                if s in DOWN_SH:
                    q = DOWN_SH[s]
                    pe.wait_ge(s_hs, 2 * q + 2)
                    down(sw2_sb[:, q, :], hid_sh[:, q % 2, :], q == 0, False)
                if s in SPREAD:
                    first = 2 * SPREAD[s]
                    if first == 0:
                        take_back(pe, s_gate, 1)
                        pe.wait_ge(s_hs, 2 * NQ - 1)
                    else:
                        pe.wait_ge(s_hr, max(e + 1 for e, at in enumerate(ROUTED) if at < s))
                    for ex in (first, first + 1):
                        mm(gb_ps[ex % 4], gfull[:, ex:ex + 1].broadcast_to([P, P]), eye_sb[:], start=True, stop=True)
                if s in UP_R0:
                    ex = UP_R0[s]
                    if ex >= 1:
                        pe.wait_ge(s_hr, ex)
                    else:
                        pe.wait_ge(s_hs, 2 * NQ)
                    product(up_rt[:, 0:TT], rw1_sb, ex * HR)
                if s in UP_R1:
                    ex = UP_R1[s]
                    product(up_rt[:, TT:2 * TT], rw1_sb, ex * HR + P).then_inc(s_up, 1)
                for step, half_of in ((DOWN_R0, 0), (DOWN_R1, 1)):
                    if s in step:
                        ex = step[s]
                        pe.wait_ge(s_hr, ex + 1)
                        last = down(rw2_sb[:, ex * RC + half_of, :], hid_rt[:, ex % 2, half_of, :], False, s == LAST)
                        if s == LAST:
                            last.then_inc(s_dn, 1)
                if with_xw:
                    if s == 0:
                        take_back(pe, s_xpart, 1)
                    for m, c, j in XW.get(s, []):
                        first, final = (c, j) == (0, 0), (c, j) == (KC - 1, len(TERMS) - 1)
                        if first and m > MF:
                            pe.wait_ge(s_xwe, m - MF)
                        of_w, of_x = TERMS[j]
                        last = mm(xw_next[:, 0:TT], wx_part[of_w][:, c, m * P:(m + 1) * P], x_part[of_x][:, c, :],
                                  start=first, stop=final)
                        if final:
                            last.then_inc(s_xwp, 1)

            pe.wait_ge(s_lw, 32)
            for m in range(MC):
                for c in range(KC):
                    last = mm(acc_lg[:, m * B:(m + 1) * B], wh_sb[:, c, m * P:(m + 1) * P],
                              cond_sb[:, c * B:(c + 1) * B], start=(c == 0), stop=(c == KC - 1))
            last.then_inc(s_xwp0, 1)
            pe.wait_ge(s_xw0, 48)
            for m in range(MC):
                if m >= len(first_banks):
                    pe.wait_ge(s_xwc0, m - len(first_banks) + 1)
                for c in range(KC):
                    last = mm(first_banks[m % len(first_banks)][:, 0:TT], wx_sb[:, c, m * P:(m + 1) * P], x_sb[:, c, 0:TT],
                              start=(c == 0), stop=(c == KC - 1))
                last.then_inc(s_xwp0, 1)
            pe.wait_ge(s_in, 16 * 4)
            pe.wait_ge(s_cond, 1)
            for c in range(KC):
                last = mm(logits, cexp[:, c, :], wr_sb[:, KC + c, :], start=(c == 0), stop=(c == KC - 1))
            last.then_inc(s_lg, 1)
            def lstm(s):
                pe.wait_ge(s_hhi, s + 1)
                low(f_ps, 4, 2)
                low(gi_ps, 0, 4)
                pe.wait_ge(s_hlo, s + 1)
                high(f_ps, 4, 2).then_inc(s_mul, 1)
                high(gi_ps, 0, 4).then_inc(s_mul, 1)
                low(o_ps, 6, 2)
                high(o_ps, 6, 2).then_inc(s_mul, 1)

            def first_tile(s):
                if s < len(XW_FIRST):
                    n, m = XW_FIRST[s]
                    if s >= 2:
                        pe.wait_ge(s_xwe, s - 1)
                    for c in range(KC):
                        last = mm(xw_first[s % 2], wx_sb[:, c, m * P:(m + 1) * P], x_sb[:, c, n * TT:(n + 1) * TT],
                                  start=(c == 0), stop=(c == KC - 1))
                    last.then_inc(s_xwp, 1)

            pe.wait_ge(s_lo, 2)
            for s in range(TS):
                lstm(s)
                if s == 0:
                    pe.wait_ge(s_x, 16)
                first_tile(s)
            take_back(pe, s_hhi, TS)
            take_back(pe, s_hlo, TS)
            take_back(pe, s_xwe, len(XW_FIRST))
            pe.wait_ge(s_mw, 16 * 5)
            pe.wait_ge(s_lo, 2 + len(LO_OF))
            with pe.Fori(1, NT):
                for s in range(TS):
                    lstm(s)
                    mixture(s, True)
                take_back(pe, s_hhi, TS)
                take_back(pe, s_hlo, TS)
                take_back(pe, s_xwe, MC - MF)
                take_back(pe, s_hs, 2 * NQ)
                take_back(pe, s_hr, NE)
            for s in range(LAST + 1):
                mixture(s, False)


def kernel(x, cond_1024, L0_cond_Wx, L0_cond_Wh, L0_cond_b, L1_cond_W_router, L1_cond_router_bias,
           L1_cond_s_w1, L1_cond_s_w3, L1_cond_s_w2, L1_cond_r_w1, L1_cond_r_w2):
    import concourse.bacc as bacc
    from concourse.bass_utils import run_bass_kernel_spmd

    def rows(a):
        a = np.asarray(a)
        return np.ascontiguousarray(a.reshape(a.shape[0] // P, P, -1).transpose(1, 0, 2))

    def gate_order(a):
        a = np.asarray(a)
        return np.concatenate([a[..., 3 * D:], a[..., :3 * D]], axis=-1)

    s_w1, s_w3, s_w2, r_w1, r_w2 = (np.asarray(a) for a in (L1_cond_s_w1, L1_cond_s_w3, L1_cond_s_w2, L1_cond_r_w1, L1_cond_r_w2))
    arrays = {
        "xT": rows(np.asarray(x).transpose(2, 1, 0).reshape(D, NTOK)),
        "condT": rows(np.asarray(cond_1024).T).reshape(P, HC),
        "wx": rows(gate_order(L0_cond_Wx)),
        "wh": rows(gate_order(L0_cond_Wh)),
        "bT": np.ascontiguousarray(gate_order(L0_cond_b).reshape(MC, P).T),
        "wr": rows(np.asarray(L1_cond_W_router).T),
        "rb": np.ascontiguousarray(np.broadcast_to(np.asarray(L1_cond_router_bias), (P, NE))),
        "sw1": rows(s_w1.reshape(FSH, D).T),
        "sw3": rows(s_w3.reshape(FSH, D).T),
        "sw2": rows(s_w2.transpose(0, 2, 1).reshape(FSH, D)),
        "rw1": rows(r_w1.reshape(NE * HR, D).T),
        "rw2": rows(r_w2.transpose(0, 2, 1).reshape(NE * HR, D)),
        "eye": np.eye(P, dtype=np.float32),
        "iota": np.ascontiguousarray(np.broadcast_to(np.arange(NE, dtype=np.float32), (P, NE))),
    }
    nc = bacc.Bacc("TRN2", target_bir_lowering=False, num_devices=1)
    args = [nc.dram_tensor(n, a.shape, mybir.dt.from_np(a.dtype), kind="ExternalInput").ap() for n, a in arrays.items()]
    args.append(nc.dram_tensor("outT", (P, KC, NTOK), F32, kind="ExternalOutput").ap())
    cond_resid_kernel(nc, *args)
    r = run_bass_kernel_spmd(nc, [arrays], core_ids=[0])
    got = r.results[0]["outT"]
    return np.ascontiguousarray(got.transpose(1, 0, 2).reshape(D, T, B).transpose(2, 1, 0))
```
